# Optimizing a Trainium2 kernel written in Bass

```python
import numpy as np
import jax
import jax.numpy as jnp

def _softmax(x, axis=-1):
    return jax.nn.softmax(x, axis=axis)

def _gelu(x):
    return jax.nn.gelu(x, approximate=True)

def _silu(x):
    return jax.nn.silu(x)

def _sigmoid(x):
    return jax.nn.sigmoid(x)

def _layernorm(x, axis=-1, eps=1e-05):
    m = jnp.mean(x, axis=axis, keepdims=True)
    v = jnp.var(x, axis=axis, keepdims=True)
    return (x - m) / jnp.sqrt(v + eps)

def _scatter_add(tgt, idx, src, axis=0):
    return tgt.at[idx].add(src)

def _segment_sum(src, seg, n):
    return jax.ops.segment_sum(src, seg, n)
kernel_name = 'mk_vit_tower_cls_d1_tok_img1024_r4_31ead9'

def setup_inputs(seed: int=0):
    np.random.seed(seed)
    _w = jnp.asarray

    def _rec_inputs():
        import jax
        import jax.numpy as jnp
        _rk = jax.random.key(seed)
        x = -0.00016672 + 0.999947 * jax.random.normal(jax.random.fold_in(_rk, 1), (16, 3, 96, 96), jnp.float32)
        cls_tok = 0.02 * jax.random.normal(jax.random.fold_in(_rk, 5), (1, 1, 256), jnp.float32)
        return (x, cls_tok)
    x, cls_tok = _rec_inputs()

    def _L0_tok_setup():
        import jax, jax.numpy as jnp
        import numpy as np
        B, C, H, W = (64, 3, 96, 96)
        P = 16
        HP, WP = (H // P, W // P)
        N = HP * WP
        F = C * P * P
        D = 256
        key = jax.random.key(seed)
        k1, k2, k3, k4, k5 = jax.random.split(key, 5)
        data = jax.random.normal(k1, (B, C, H, W), dtype=jnp.float32)
        lim = 1.0 / np.sqrt(F)
        W_lin = jax.random.uniform(k2, (D, F), minval=-lim, maxval=lim, dtype=jnp.float32)
        b_lin = jax.random.uniform(k3, (D,), minval=-lim, maxval=lim, dtype=jnp.float32)
        class_token = jax.random.normal(k4, (1, 1, D), dtype=jnp.float32)
        position_embeddings = jax.random.normal(k5, (1, N + 1, D), dtype=jnp.float32)
        return {'data': data, 'W_lin': W_lin, 'b_lin': b_lin, 'class_token': class_token, 'position_embeddings': position_embeddings}
    _L0_tok_all = _L0_tok_setup()
    _L0_tok_in = {k: v for k, v in _L0_tok_all.items() if k in ('W_lin', 'b_lin', 'class_token', 'position_embeddings')}
    del _L0_tok_all

    def _L0_attn_setup():
        import jax, jax.numpy as jnp
        import numpy as np
        B, T, EMB, HEADS = (4, 512, 256, 16)
        CHUNK = EMB // HEADS
        key = jax.random.key(seed)
        kx, kq, kk, kv, ku = jax.random.split(key, 5)
        s = CHUNK ** (-0.5)
        return {'x': jax.random.normal(kx, (B, T, EMB), jnp.float32), 'Wq': jax.random.normal(kq, (CHUNK, CHUNK), jnp.float32) * s, 'Wk': jax.random.normal(kk, (CHUNK, CHUNK), jnp.float32) * s, 'Wv': jax.random.normal(kv, (CHUNK, CHUNK), jnp.float32) * s, 'Wu': jax.random.normal(ku, (EMB, EMB), jnp.float32) * EMB ** (-0.5), 'bu': jnp.zeros((EMB,), jnp.float32)}
    _L0_attn_all = _L0_attn_setup()
    _L0_attn_in = {k: v for k, v in _L0_attn_all.items() if k in ('Wq', 'Wk', 'Wv', 'Wu', 'bu')}
    del _L0_attn_all

    def _L0_ffn_setup():
        import jax, jax.numpy as jnp
        import numpy as np
        DIM = 256
        NUM_EXPERTS = 8
        HIDDEN = 1024
        CAP_FACTOR = 2.0
        B, S = (4, 512)
        key = jax.random.key(seed)
        ks = jax.random.split(key, 6)
        scale_r = 1.0 / np.sqrt(DIM)
        scale_1 = 1.0 / np.sqrt(DIM)
        scale_2 = 1.0 / np.sqrt(HIDDEN)
        return {'x': jax.random.normal(ks[0], (B, S, DIM), dtype=jnp.float32), 'router_w': jax.random.uniform(ks[1], (NUM_EXPERTS, DIM), jnp.float32, -scale_r, scale_r), 'w1': jax.random.uniform(ks[2], (NUM_EXPERTS, DIM, HIDDEN), jnp.float32, -scale_1, scale_1), 'b1': jax.random.uniform(ks[3], (NUM_EXPERTS, HIDDEN), jnp.float32, -scale_1, scale_1), 'w2': jax.random.uniform(ks[4], (NUM_EXPERTS, HIDDEN, DIM), jnp.float32, -scale_2, scale_2), 'b2': jax.random.uniform(ks[5], (NUM_EXPERTS, DIM), jnp.float32, -scale_2, scale_2)}
    _L0_ffn_all = _L0_ffn_setup()
    _L0_ffn_in = {k: v for k, v in _L0_ffn_all.items() if k in ('router_w', 'w1', 'b1', 'w2', 'b2')}
    del _L0_ffn_all
    return {'x': x, 'cls_tok': cls_tok, 'L0_tok_W_lin': _L0_tok_in['W_lin'], 'L0_tok_b_lin': _L0_tok_in['b_lin'], 'L0_tok_class_token': _L0_tok_in['class_token'], 'L0_tok_position_embeddings': _L0_tok_in['position_embeddings'], 'L0_attn_Wq': _L0_attn_in['Wq'], 'L0_attn_Wk': _L0_attn_in['Wk'], 'L0_attn_Wv': _L0_attn_in['Wv'], 'L0_attn_Wu': _L0_attn_in['Wu'], 'L0_attn_bu': _L0_attn_in['bu'], 'L0_ffn_router_w': _L0_ffn_in['router_w'], 'L0_ffn_w1': _L0_ffn_in['w1'], 'L0_ffn_b1': _L0_ffn_in['b1'], 'L0_ffn_w2': _L0_ffn_in['w2'], 'L0_ffn_b2': _L0_ffn_in['b2']}

def reference(x, cls_tok, L0_tok_W_lin, L0_tok_b_lin, L0_tok_class_token, L0_tok_position_embeddings, L0_attn_Wq, L0_attn_Wk, L0_attn_Wv, L0_attn_Wu, L0_attn_bu, L0_ffn_router_w, L0_ffn_w1, L0_ffn_b1, L0_ffn_w2, L0_ffn_b2):
    import jax
    import jax.numpy as jnp

    def _L0_tok_ref(data, W_lin, b_lin, class_token, position_embeddings):
        import jax, jax.numpy as jnp
        import numpy as np
        B, C, H, W = (64, 3, 96, 96)
        P = 16
        HP, WP = (H // P, W // P)
        N = HP * WP
        F = C * P * P
        D = 256
        b = data.shape[0]
        x = data.reshape(b, C, HP, P, WP, P)
        x = x.transpose(0, 2, 4, 1, 3, 5).reshape(b, N, F)
        x = jnp.einsum('bnf,df->bnd', x, W_lin) + b_lin
        cls = jnp.broadcast_to(class_token, (b, 1, D))
        out = jnp.concatenate([cls, x], axis=1) + position_embeddings
        return out

    def _L0_attn_ref(x, Wq, Wk, Wv, Wu, bu):
        import jax, jax.numpy as jnp
        import numpy as np
        B, T, EMB, HEADS = (4, 512, 256, 16)
        CHUNK = EMB // HEADS
        b, t, d = x.shape
        h = HEADS
        c = d // h
        xh = x.reshape(b, t, h, c)
        scale = d ** (-0.25)
        q = jnp.einsum('bthc,oc->btho', xh, Wq) * scale
        k = jnp.einsum('bthc,oc->btho', xh, Wk) * scale
        v = jnp.einsum('bthc,oc->btho', xh, Wv)
        scores = jnp.einsum('bihc,bjhc->bhij', q, k)
        i = jnp.arange(t)[:, None]
        j = jnp.arange(t)[None, :]
        scores = jnp.where(j > i, -jnp.inf, scores)
        attn = jax.nn.softmax(scores, axis=-1)
        y = jnp.einsum('bhij,bjhc->bihc', attn, v).reshape(b, t, d)
        return y @ Wu.T + bu

    def _L0_ffn_ref(x, router_w, w1, b1, w2, b2):
        import jax, jax.numpy as jnp
        import numpy as np
        DIM = 256
        NUM_EXPERTS = 8
        HIDDEN = 1024
        CAP_FACTOR = 2.0
        B, S = (4, 512)
        Bz, Sz, Dz = x.shape
        E = router_w.shape[0]
        capacity = max(1, int(Sz * CAP_FACTOR / E) + 1)
        scores = jax.nn.softmax(jnp.einsum('bsd,ed->bse', x, router_w), axis=-1)
        scores_t = jnp.swapaxes(scores, 1, 2)
        gate_vals, sel_idx = jax.lax.top_k(scores_t, capacity)
        b_idx = jnp.arange(Bz)[:, None, None]
        tokens = x[b_idx, sel_idx]
        h = jnp.einsum('becd,edh->bech', tokens, w1) + b1[None, :, None, :]
        h = jax.nn.gelu(h, approximate=False)
        y = jnp.einsum('bech,ehd->becd', h, w2) + b2[None, :, None, :]
        gated = y * gate_vals[..., None]
        out = jnp.zeros_like(x).at[b_idx, sel_idx].add(gated)
        return out
    h = _L0_tok_ref(x, L0_tok_W_lin, L0_tok_b_lin, L0_tok_class_token, L0_tok_position_embeddings)
    h = jnp.concatenate([jnp.broadcast_to(cls_tok, (h.shape[0], 1, h.shape[2])), h], axis=1)
    h = h + _L0_attn_ref(_layernorm(h, axis=-1), L0_attn_Wq, L0_attn_Wk, L0_attn_Wv, L0_attn_Wu, L0_attn_bu)
    h = h + _L0_ffn_ref(_layernorm(h, axis=-1), L0_ffn_router_w, L0_ffn_w1, L0_ffn_b1, L0_ffn_w2, L0_ffn_b2)
    return h

_drawn_inputs = setup_inputs


def setup_inputs(seed=0):
    import zlib

    import numpy as np

    out = dict(_drawn_inputs(seed))
    spreads = {'L0_attn_bu': (0.0, 0.1)}
    factors = {'L0_ffn_b1': 8.0, 'L0_ffn_b2': 8.0}
    for name, (base, spread) in spreads.items():
        noise = np.random.default_rng([zlib.crc32(name.encode()), seed]).standard_normal(out[name].shape)
        drawn = base * np.exp(spread * noise) if base else spread * noise
        out[name] = jnp.asarray(drawn.astype(out[name].dtype))
    for name, factor in factors.items():
        out[name] = (out[name] * factor).astype(out[name].dtype)
    return out
```

```python
from contextlib import ExitStack

import concourse.bass as bass
from concourse import mybir

B, C_IN, IMG, PATCH = 16, 3, 96, 16
D, HEADS, HC = 256, 16, 16
NPATCH = (IMG // PATCH) ** 2
S = NPATCH + 2
TOK = B * S
F = C_IN * PATCH * PATCH
KF = F // 128
E, HID = 8, 1024
NH = HID // 128
CAP = max(1, int(S * 2.0 / E) + 1)
SLOTS = B * CAP

GB = 3
GT = GB * S
G = -(-B // GB)
GTP = G * GT
PAIRS = B // 2
UNITS = G // 2
QPAD = TOK + 64 - S
POS = 18
TRIPLES = POS // 3
VC = HC + 1
NBUF = 4
MASKED = -1e30

C_ID, C_KM, C_M3, C_PAT, C_ZM, C_D38, C_LM, C_E8, C_I64 = 0, 128, 132, 148, 178, 181, 219, 237, 245
C_CM = C_I64 + 64
C_END = C_CM + 8 * S


def rows(g):
    return min(GT, TOK - g * GT)


def pics(g):
    return min(GB, B - g * GB)


def tower(nc, xp, wl, rows_a, rows_b, bd, wu, bu, rw, w1, b1, w2, b2, consts, out):
    fp32, bf16 = mybir.dt.float32, mybir.dt.bfloat16
    ALU, ACT, AX = mybir.AluOpType, mybir.ActivationFunctionType, mybir.AxisListType

    with ExitStack() as ctx:
        def sb(name, shape, dt=fp32):
            return ctx.enter_context(nc.sbuf_tensor(name, shape, dt))

        def sem(name):
            return ctx.enter_context(nc.semaphore(name))

        const = sb("const", [128, C_END])
        ident = const[:, C_ID:C_ID + 128]
        constb = sb("constb", [128, C_END - C_E8], bf16)
        e8b = constb[:, 0:8]
        id64b = constb[:, C_I64 - C_E8:C_I64 - C_E8 + 64]
        causalb = constb[:, C_CM - C_E8:C_CM - C_E8 + 8 * S]
        xps = sb("xps", [128, KF * TOK])
        wls = sb("wls", [128, KF, D])
        add_a = sb("add_a", [128, D])
        add_b = sb("add_b", [128, D])
        bds = sb("bds", [128, 3, 128])
        wus = sb("wus", [128, 2, D])
        bus = sb("bus", [128, D])
        rws = sb("rws", [128, 2, E])
        b1s = sb("b1s", [128, E * NH])
        b2s = sb("b2s", [128, E * 2])
        w1s = sb("w1s", [128, NBUF, 2, HID])
        w2s = sb("w2s", [128, NBUF, NH, D])
        h = sb("h", [128, G, D])
        hb = sb("hb", [128, G, D])
        xn = sb("xn", [128, G, D])
        stat = sb("stat", [128, G, 6])
        mv = sb("mv", [128, G, 2])
        ve = sb("ve", [128, G])
        lnv = sb("lnv", [128, G])
        r0 = sb("r0", [128, G])
        nt = sb("nt", [128, G, 2])
        rstd = sb("rstd", [128, G])
        xnT = sb("xnT", [128, 2, GTP])
        qT = sb("qT", [128, 2, QPAD])
        kf = sb("kf", [128, 2, 2, 2 * GT])
        km = sb("km", [128, 2, 4, TOK])
        vb = sb("vb", [128, 2, 2, HEADS, VC])
        mx = sb("mx", [128, 2, HEADS])
        pr = sb("pr", [128, 2, POS, S])
        pT = sb("pT", [128, 2, TRIPLES, 128])
        rs = sb("rs", [128, 2, HEADS])
        ys = sb("ys", [128, 2, HEADS, HC])
        yT = sb("yT", [128, 2, TOK])
        rmax = sb("rmax", [128, G])
        lsh = sb("lsh", [128, G, E])
        lex = sb("lex", [128, G, E])
        rsum = sb("rsum", [128, G])
        rrec = sb("rrec", [128, G])
        sc = sb("sc", [128, G, E])
        zr = sb("zr", [128, G, 128])
        rv = sb("rv", [128, S])
        rv2 = sb("rv2", [128, S])
        top = sb("top", [128, 2, 8])
        isgt = sb("isgt", [128, S])
        ngt = sb("ngt", [128, 1])
        iseq = sb("iseq", [128, S])
        ceq = sb("ceq", [128, S])
        fits = sb("fits", [128, S])
        picked = sb("picked", [128, S])
        cpick = sb("cpick", [128, S])
        slot = sb("slot", [128, S])
        lall = sb("lall", [128, G * GB, S], bf16)
        shared = sb("shared", [128, 2 * B * GT])
        xn3 = shared[:, :].rearrange("p (c b r) -> p c b r", c=2, b=B)
        sel = shared[:, 0:G * E * GB * CAP].rearrange("p (g s) -> p g s", g=G)
        selg = shared[:, G * E * GB * CAP:2 * G * E * GB * CAP].rearrange("p (g s) -> p g s", g=G)
        sgT = sb("sgT", [128, 2, G, GT])
        tokT = sb("tokT", [128, 2, E, SLOTS])
        gT = km[:].rearrange("p c m t -> p (c m t)")[:, 0:2 * NH * SLOTS].rearrange("p (b k s) -> p b k s", b=2, k=NH)
        yeT = xps[:, 0:2 * E * SLOTS].rearrange("p (c q s) -> p c q s", c=2, q=2)
        yq = wls
        ob = hb

        bank = [ctx.enter_context(nc.psum_tensor(f"bank{i}", [128, 512], fp32)) for i in range(8)]

        in_wl, in_const, in_rows, in_bd, in_wu, in_bu, in_rw, in_b = (
            sem(n) for n in ("in_wl", "in_const", "in_rows", "in_bd", "in_wu", "in_bu", "in_rw", "in_b"))
        in_xp = [sem(f"in_xp{g}") for g in range(G)]
        in_w1 = [sem(f"in_w1_{i}") for i in range(NBUF)]
        in_w2 = [sem(f"in_w2_{i}") for i in range(NBUF)]
        (constb_ready, rows_ready, fills_done, hb_done, selg_done, xn3_done) = (
            sem(n) for n in ("constb_ready", "rows_ready", "fills_done", "hb_done", "selg_done", "xn3_done"))
        (patch_done, xnt_ps, q_ps, k_ps, v_ps, s_ps, pt_ps, pv_ps, yt_ps, o_ps, logit_ps, route_ps, slot_ps,
         gather_ps, sgt_ps, f1_ps, f2_ps, yq_ps, sc_ps) = (
            sem(n) for n in ("patch_done", "xnt_ps", "q_ps", "k_ps", "v_ps", "s_ps", "pt_ps", "pv_ps", "yt_ps",
                             "o_ps", "logit_ps", "route_ps", "slot_ps", "gather_ps", "sgt_ps", "f1_ps", "f2_ps",
                             "yq_ps", "sc_ps"))
        (h_done, stats_done, mv_done, ve_done, nt_done, rstd_done, xn_done, km_done, vb_done, mx_done, sub_done,
         rs_done, y_done, soft_done, lsh_done, sc_done, z_done, topk_done, lall_done, sel_done, sgt_done, ye_done,
         ob_done) = (
            sem(n) for n in ("h_done", "stats_done", "mv_done", "ve_done", "nt_done", "rstd_done", "xn_done",
                             "km_done", "vb_done", "mx_done", "sub_done", "rs_done", "y_done", "soft_done",
                             "lsh_done", "sc_done", "z_done", "topk_done", "lall_done", "sel_done", "sgt_done",
                             "ye_done", "ob_done"))
        (ln_done, r0_done, xnt_done, q_done, k_done, exp_done, pt_done, yt_done, lex_done, gather_act,
         gather_dve, gelu_done, yq_act, yq_dve) = (
            sem(n) for n in ("ln_done", "r0_done", "xnt_done", "q_done", "k_done", "exp_done", "pt_done", "yt_done",
                             "lex_done", "gather_act", "gather_dve", "gelu_done", "yq_act", "yq_dve"))
        stored = sem("stored")

        def yq_bank(q, g):
            return 6 if q == 0 else g % 4

        def sc_bank(q, g):
            return 7 if q == 0 else 6 + g % 2

        block = ctx.enter_context(nc.Block())

        @block.sync
        def _(sp):
            sp.dma_start(wls[:], wl).then_inc(in_wl, 16)
            for g in range(G):
                a = KF * GT * g
                sp.dma_start(xps[:, a:a + KF * rows(g)], xp[:, a:a + KF * rows(g)]).then_inc(in_xp[g], 16)
            for e in range(E):
                if e >= NBUF:
                    sp.wait_ge(f1_ps, NH * (e - NBUF + 1))
                sp.dma_start(w1s[:, e % NBUF, :, :], w1[e, :, :, :]).then_inc(in_w1[e % NBUF], 16)
                if e >= NBUF:
                    sp.wait_ge(f2_ps, 2 * (e - NBUF + 1))
                sp.dma_start(w2s[:, e % NBUF, :, :], w2[e, :, :, :]).then_inc(in_w2[e % NBUF], 16)
            for g in range(G):
                sp.wait_ge(ob_done, G + g + 1)
                sp.dma_start(out[g * GT:g * GT + rows(g), :], ob[0:rows(g), g, :]).then_inc(stored, 16)
            sp.wait_ge(stored, 16 * G)

        @block.gpsimd
        def _(pool):
            pool.dma_start(wus[:], wu).then_inc(in_wu, 16)
            pool.dma_start(rws[:], rw).then_inc(in_rw, 16)
            pool.dma_start(b1s[:], b1).then_inc(in_b, 16)
            pool.dma_start(b2s[:], b2).then_inc(in_b, 16)
            pool.wait_ge(in_rows, 32)
            nc.gpsimd.tensor_tensor(add_a[:], add_a[:], add_b[:], ALU.add).then_inc(rows_ready, 1)
            nc.gpsimd.memset(qT[:, :, TOK:QPAD], 0.0).then_inc(fills_done, 1)
            nc.gpsimd.memset(pr[:, :, HEADS:POS, :], 0.0).then_inc(fills_done, 1)
            pool.wait_ge(in_const, 16)
            nc.gpsimd.tensor_copy(constb[:], const[:, C_E8:C_END]).then_inc(constb_ready, 1)
            nc.gpsimd.tensor_copy(
                vb[:, :, :, :, HC], const[:, C_M3:C_M3 + HEADS].unsqueeze(1).unsqueeze(1).to_broadcast([128, 2, 2, HEADS])
            ).then_inc(fills_done, 1)
            nc.gpsimd.memset(zr[:], 0.0).then_inc(fills_done, 1)
            pool.wait_ge(in_bu, 16)
            for g in range(G + 2):
                if g >= 2:
                    k = g - 2
                    pool.wait_ge(xnt_done, k + 1)
                    for c in range(2):
                        last = nc.gpsimd.tensor_copy(
                            xn3[:, c, k * GB:k * GB + pics(k), :].rearrange("p b (r t) -> p b r t", r=3),
                            xnT[:, c, k * GT:k * GT + rows(k)].rearrange("p (b t) -> p b t", t=S).unsqueeze(2)
                            .to_broadcast([128, pics(k), 3, S]))
                    last.then_inc(xn3_done, 1)
                if g == G or g == G + 1:
                    continue
                pool.wait_ge(h_done, g + 1)
                nc.gpsimd.tensor_tensor(hb[0:rows(g), g, :], h[0:rows(g), g, :], bus[0:rows(g), :],
                                        ALU.add).then_inc(hb_done, 1)
            pool.wait_ge(v_ps, PAIRS)
            nc.gpsimd.memset(xnT[:, :, TOK:GTP], 0.0).then_inc(fills_done, 1)
            for g in range(G):
                pool.wait_ge(sel_done, g + 1)
                n = pics(g) * CAP
                nc.gpsimd.tensor_tensor(
                    selg[0:rows(g), g, 0:E * n].rearrange("p (e s) -> p e s", e=E),
                    sel[0:rows(g), g, 0:E * n].rearrange("p (e s) -> p e s", e=E),
                    sc[0:rows(g), g, :].unsqueeze(2).to_broadcast([rows(g), E, n]), ALU.mult).then_inc(selg_done, 1)

        @block.scalar
        def _(act):
            act.dma_start(add_a[:], rows_a).then_inc(in_rows, 16)
            act.dma_start(add_b[:], rows_b).then_inc(in_rows, 16)
            act.dma_start(const[:], consts).then_inc(in_const, 16)
            act.dma_start(bds[:], bd).then_inc(in_bd, 16)
            act.dma_start(bus[:], bu).then_inc(in_bu, 16)
            nc.scalar.preload_act_table_set("natural_log_exp_and_others")

            def first_rstd(g, norm):
                n = rows(g)
                act.wait_ge(ve_done, norm * G + g + 1)
                nc.scalar.activation(lnv[0:n, g:g + 1], ve[0:n, g:g + 1], ACT.Ln).then_inc(ln_done, 1)
                act.wait_ge(ln_done, norm * G + g + 1)
                nc.scalar.activation(r0[0:n, g:g + 1], lnv[0:n, g:g + 1], ACT.Exp, scale=-0.5).then_inc(r0_done, 1)

            def take_xnT(g, norm):
                n = rows(g)
                act.wait_ge(xnt_ps, norm * G + g + 1)
                nc.scalar.activation(xnT[:, :, g * GT:g * GT + n],
                                     bank[2 + g % 2][:, 0:2 * n].rearrange("p (c t) -> p c t", c=2),
                                     ACT.Copy).then_inc(xnt_done, 1)

            def take_qk(u):
                n = min(2 * GT, TOK - 2 * GT * u)
                t0 = 2 * GT * u
                act.wait_ge(q_ps, u + 1)
                nc.scalar.activation(qT[:, :, t0:t0 + n],
                                     bank[4 + 2 * (u % 2)][:, 0:2 * n].rearrange("p (c t) -> p c t", c=2),
                                     ACT.Copy, scale=0.25).then_inc(q_done, 1)
                act.wait_ge(k_ps, u + 1)
                if u >= 2:
                    act.wait_ge(km_done, 4 * (u - 1))
                nc.scalar.activation(kf[:, u % 2, :, 0:n],
                                     bank[5 + 2 * (u % 2)][:, 0:2 * n].rearrange("p (c t) -> p c t", c=2),
                                     ACT.Copy).then_inc(k_done, 1)

            for g in range(G):
                first_rstd(g, 0)
                if g >= 2:
                    take_xnT(g - 2, 0)
                if g == 3:
                    take_qk(0)
                if g == 5:
                    take_qk(1)
            take_xnT(4, 0)
            take_xnT(5, 0)
            take_qk(2)

            def take_pT(p):
                act.wait_ge(pt_ps, p + 1)
                if p >= 2:
                    act.wait_ge(pv_ps, p - 1)
                nc.scalar.activation(pT[0:GT, p % 2, 0:4, :],
                                     bank[4][0:GT, :].rearrange("p (t n) -> p t n", t=4), ACT.Copy).then_inc(pt_done, 1)
                nc.scalar.activation(pT[0:GT, p % 2, 4:6, :],
                                     bank[5][0:GT, 0:256].rearrange("p (t n) -> p t n", t=2),
                                     ACT.Copy).then_inc(pt_done, 1)

            def take_yT(p):
                act.wait_ge(yt_ps, p + 1)
                nc.scalar.activation(
                    yT[:, :, 2 * p * S:2 * (p + 1) * S].rearrange("p c (b t) -> p c b t", b=2),
                    bank[7][:, 0:256].rearrange("p (c b t) -> p c b t", c=2, b=2)[:, :, :, 0:S],
                    ACT.Copy).then_inc(yt_done, 1)

            def weights(p):
                act.wait_ge(sub_done, p + 1)
                nc.scalar.activation(pr[:, p % 2, 0:HEADS, :], pr[:, p % 2, 0:HEADS, :], ACT.Exp).then_inc(exp_done, 1)

            for p in range(PAIRS + 2):
                if p >= 2:
                    take_yT(p - 2)
                if 1 <= p <= PAIRS:
                    take_pT(p - 1)
                if p < PAIRS:
                    weights(p)

            for g in range(G + 2):
                if g < G:
                    first_rstd(g, 1)
                if g >= 2:
                    take_xnT(g - 2, 1)
            act.wait_ge(lsh_done, 2)
            for part, (n, a, b) in enumerate(((GT, 0, G - 1), (rows(G - 1), G - 1, G))):
                nc.scalar.activation(lex[0:n, a:b, :], lsh[0:n, a:b, :], ACT.Exp).then_inc(lex_done, 1)
            for g in range(0, G, 2):
                act.wait_ge(gather_ps, g + 1)
                n = pics(g) * CAP
                nc.scalar.activation(tokT[:, :, :, g * GB * CAP:g * GB * CAP + n],
                                     bank[g % 4][:, 0:2 * E * n].rearrange("p (c e s) -> p c e s", c=2, e=E),
                                     ACT.Copy).then_inc(gather_act, 1)

            def take_yq(q, g):
                i = q * G + g
                act.wait_ge(yq_ps, i + 1)
                if i >= 6:
                    act.wait_ge(sc_ps, i - 5)
                n = 4 * pics(g) * CAP
                nc.scalar.activation(yq[0:n, i % 6, :], bank[yq_bank(q, g)][0:n, 0:D], ACT.Copy).then_inc(yq_act, 1)

            act.wait_ge(in_b, 32)
            for e in range(E):
                if e >= 2:
                    act.wait_ge(f2_ps, 2 * (e - 1))
                for c in range(NH):
                    i = e * NH + c
                    act.wait_ge(f1_ps, i + 1)
                    nc.scalar.activation(gT[:, e % 2, c, :], bank[i % 4][:, 0:SLOTS], ACT.Gelu,
                                         bias=b1s[:, i:i + 1]).then_inc(gelu_done, 1)
            for g in range(0, G, 2):
                take_yq(1, g)

        @block.vector
        def _(dve):
            def norm_stats(g, norm):
                n = rows(g)
                k = norm * G + g + 1
                if norm == 0:
                    dve.wait_ge(patch_done, g + 1)
                    dve.wait_ge(rows_ready, 1)
                    nc.vector.tensor_tensor(h[0:n, g, :], bank[g % 2][0:n, 0:D], add_a[0:n, :], ALU.add).then_inc(h_done, 1)
                else:
                    dve.wait_ge(o_ps, g + 1)
                    dve.wait_ge(hb_done, g + 1)
                    nc.vector.tensor_tensor(h[0:n, g, :], bank[g % 2][0:n, 0:D], hb[0:n, g, :], ALU.add).then_inc(h_done, 1)
                dve.wait_ge(h_done, k)
                nc.vector.bn_stats(stat[0:n, g, :], h[0:n, g, :]).then_inc(stats_done, 1)
                dve.wait_ge(stats_done, k)
                nc.vector.bn_aggr(mv[0:n, g, :], stat[0:n, g, :]).then_inc(mv_done, 1)
                dve.wait_ge(mv_done, k)
                nc.vector.tensor_scalar(ve[0:n, g:g + 1], mv[0:n, g, 1:2], 1e-5, None, ALU.add).then_inc(ve_done, 1)

            def norm_apply(g, norm):
                n = rows(g)
                k = norm * G + g + 1
                dve.wait_ge(r0_done, k)
                nc.vector.scalar_tensor_tensor(nt[0:n, g, 0:1], r0[0:n, g:g + 1], ve[0:n, g:g + 1], r0[0:n, g:g + 1],
                                               ALU.mult, ALU.mult).then_inc(nt_done, 1)
                dve.wait_ge(nt_done, 2 * k - 1)
                nc.vector.tensor_scalar(nt[0:n, g, 1:2], nt[0:n, g, 0:1], -0.5, 1.5, ALU.mult, ALU.add).then_inc(nt_done, 1)
                dve.wait_ge(nt_done, 2 * k)
                nc.vector.tensor_tensor(rstd[0:n, g:g + 1], r0[0:n, g:g + 1], nt[0:n, g, 1:2], ALU.mult).then_inc(rstd_done, 1)
                dve.wait_ge(rstd_done, k)
                if norm == 1:
                    dve.wait_ge(xnt_ps, G)
                dst, src = xn[0:n, g, :], h[0:n, g, :]
                if norm == 0:
                    dst = dst.rearrange("p (c f r) -> p c f r", c=2, f=2)
                    src = src.rearrange("p (f c r) -> p c f r", c=2, f=2)
                nc.vector.tensor_scalar(dst, src, mv[0:n, g, 0:1], rstd[0:n, g:g + 1],
                                        ALU.subtract, ALU.mult).then_inc(xn_done, 1)

            def spread_k(u):
                n = min(2 * GT, TOK - 2 * GT * u)
                t0 = 2 * GT * u
                dve.wait_ge(k_done, u + 1)
                for m in range(4):
                    nc.vector.tensor_scalar(km[:, :, m, t0:t0 + n], kf[:, u % 2, :, 0:n],
                                            const[:, C_KM + m:C_KM + m + 1], None, ALU.mult).then_inc(km_done, 1)

            norm_stats(0, 0)
            for g in range(1, G):
                norm_stats(g, 0)
                norm_apply(g - 1, 0)
                if g == 4:
                    spread_k(0)
            norm_apply(G - 1, 0)
            spread_k(1)
            spread_k(2)

            def take_v(p):
                dve.wait_ge(v_ps, p + 1)
                if p >= 2:
                    dve.wait_ge(pv_ps, p - 1)
                if p == 0:
                    dve.wait_ge(in_const, 16)
                nc.vector.tensor_tensor(
                    vb[0:GT, p % 2, :, :, 0:HC], bank[6][0:GT, :].rearrange("p (b h c) -> p b h c", b=2, h=HEADS),
                    const[0:GT, C_M3:C_M3 + HEADS].unsqueeze(1).unsqueeze(3).to_broadcast([GT, 2, HEADS, HC]),
                    ALU.mult).then_inc(vb_done, 1)

            def subtract_max(p):
                s = 2 * (p % 2)
                dve.wait_ge(s_ps, p + 1)
                for f in range(2):
                    nc.vector.tensor_reduce(mx[:, p % 2, 8 * f:8 * f + 8],
                                            bank[s + f][:, 0:8 * S].rearrange("p (h t) -> p h t", h=8), AX.X,
                                            ALU.max).then_inc(mx_done, 1)
                if p >= 2:
                    dve.wait_ge(pt_ps, p - 1)
                for f in range(2):
                    dve.wait_ge(mx_done, 2 * p + f + 1)
                    last = nc.vector.tensor_tensor(
                        pr[:, p % 2, 8 * f:8 * f + 8, :], bank[s + f][:, 0:8 * S].rearrange("p (h t) -> p h t", h=8),
                        mx[:, p % 2, 8 * f:8 * f + 8].unsqueeze(2).to_broadcast([128, 8, S]), ALU.subtract)
                last.then_inc(sub_done, 1)

            def divide(p):
                y = bank[7][:, 0:HEADS * VC].rearrange("p (h c) -> p h c", h=HEADS)
                dve.wait_ge(pv_ps, p + 1)
                nc.vector.reciprocal(rs[:, p % 2, :], y[:, :, HC]).then_inc(rs_done, 1)
                dve.wait_ge(rs_done, p + 1)
                if p >= 2:
                    dve.wait_ge(yt_ps, p - 1)
                nc.vector.tensor_tensor(ys[:, p % 2, :, :], y[:, :, 0:HC],
                                        rs[:, p % 2, :].unsqueeze(2).to_broadcast([128, HEADS, HC]),
                                        ALU.mult).then_inc(y_done, 1)

            for p in range(PAIRS + 1):
                if p < PAIRS:
                    take_v(p)
                    subtract_max(p)
                if p >= 1:
                    divide(p - 1)

            norm_stats(0, 1)
            for g in range(1, G):
                norm_stats(g, 1)
                norm_apply(g - 1, 1)
            norm_apply(G - 1, 1)

            parts = ((GT, 0, G - 1), (rows(G - 1), G - 1, G))
            logits = bank[4][:, 0:G * E].rearrange("p (g e) -> p g e", e=E)
            dve.wait_ge(logit_ps, G)
            for n, a, b in parts:
                nc.vector.tensor_reduce(rmax[0:n, a:b], logits[0:n, a:b, :], AX.X, ALU.max).then_inc(soft_done, 1)
            for k, (n, a, b) in enumerate(parts):
                dve.wait_ge(soft_done, k + 1)
                nc.vector.tensor_tensor(lsh[0:n, a:b, :], logits[0:n, a:b, :],
                                        rmax[0:n, a:b].unsqueeze(2).to_broadcast([n, b - a, E]),
                                        ALU.subtract).then_inc(lsh_done, 1)
            for k, (n, a, b) in enumerate(parts):
                dve.wait_ge(lex_done, k + 1)
                nc.vector.tensor_reduce(rsum[0:n, a:b], lex[0:n, a:b, :], AX.X, ALU.add).then_inc(soft_done, 1)
            for k, (n, a, b) in enumerate(parts):
                dve.wait_ge(soft_done, 3 + k)
                nc.vector.reciprocal(rrec[0:n, a:b], rsum[0:n, a:b]).then_inc(soft_done, 1)
            for k, (n, a, b) in enumerate(parts):
                dve.wait_ge(soft_done, 5 + k)
                nc.vector.tensor_tensor(sc[0:n, a:b, :], lex[0:n, a:b, :],
                                        rrec[0:n, a:b].unsqueeze(2).to_broadcast([n, b - a, E]),
                                        ALU.mult).then_inc(sc_done, 1)
            dve.wait_ge(fills_done, 4)
            for k, (n, a, b) in enumerate(parts):
                dve.wait_ge(sc_done, k + 1)
                for g in range(a, b):
                    m = pics(g)
                    last = nc.vector.tensor_tensor(
                        zr[0:n, g, g * GB * E:g * GB * E + m * E].rearrange("p (b e) -> p b e", b=m),
                        sc[0:n, g, :].unsqueeze(1).to_broadcast([n, m, E]),
                        const[0:n, C_ZM:C_ZM + m].unsqueeze(2).to_broadcast([n, m, E]), ALU.mult)
            last.then_inc(z_done, 1)

            steps = [0]

            def step(ins):
                ins.then_inc(topk_done, 1)
                steps[0] += 1
                dve.wait_ge(topk_done, steps[0])

            dve.wait_ge(route_ps, 1)
            step(nc.vector.tensor_copy(rv[:], bank[5][:, 0:S]))
            step(nc.vector.max(top[:, 0, :], rv[:]))
            step(nc.vector.match_replace(rv2[:], top[:, 0, :], rv[:], -1.0))
            step(nc.vector.max(top[:, 1, :], rv2[:]))
            least = top[:, 1, CAP - 9:CAP - 8]
            step(nc.vector.tensor_scalar(isgt[:], rv[:], least, 0.0, ALU.is_gt, ALU.add, accum_out=ngt[:]))
            step(nc.vector.tensor_scalar(iseq[:], rv[:], least, None, ALU.is_equal))
            step(nc.vector.tensor_tensor_scan(ceq[:], iseq[:], iseq[:], 0.0, ALU.add, ALU.bypass))
            step(nc.vector.tensor_scalar(fits[:], ceq[:], ngt[:], float(CAP), ALU.add, ALU.is_le))
            step(nc.vector.tensor_tensor(fits[:], fits[:], iseq[:], ALU.mult))
            step(nc.vector.tensor_tensor(picked[:], fits[:], isgt[:], ALU.add))
            step(nc.vector.tensor_tensor_scan(cpick[:], picked[:], picked[:], 0.0, ALU.add, ALU.bypass))
            step(nc.vector.tensor_tensor(slot[:], cpick[:], picked[:], ALU.mult))
            nc.vector.tensor_tensor(lall[:], slot[:].unsqueeze(1).to_broadcast([128, G * GB, S]),
                                    const[:, C_LM:C_LM + G * GB].unsqueeze(2).to_broadcast([128, G * GB, S]),
                                    ALU.mult).then_inc(lall_done, 1)
            dve.wait_ge(slot_ps, 1)
            slots = bank[6][:, 0:G * E].rearrange("p (g e) -> p g e", e=E)
            for g in range(G):
                n, m = rows(g), pics(g) * CAP
                nc.vector.tensor_tensor(sel[0:n, g, 0:E * m].rearrange("p (e s) -> p e s", e=E), slots[0:n, g, :].unsqueeze(2).to_broadcast([n, E, m]),
                                        const[0:n, C_PAT:C_PAT + m].unsqueeze(1).to_broadcast([n, E, m]),
                                        ALU.is_equal).then_inc(sel_done, 1)
            for g in range(1, G, 2):
                dve.wait_ge(gather_ps, g + 1)
                n = pics(g) * CAP
                nc.vector.tensor_copy(tokT[:, :, :, g * GB * CAP:g * GB * CAP + n],
                                      bank[g % 4][:, 0:2 * E * n].rearrange("p (c e s) -> p c e s", c=2, e=E)
                                      ).then_inc(gather_dve, 1)
            for r in range(3):
                dve.wait_ge(sgt_ps, r + 1)
                for k in range(4):
                    q, g = divmod(4 * r + k, G)
                    n, m = rows(g), 4 * pics(g) * CAP
                    last = nc.vector.tensor_copy(sgT[0:m, q, g, 0:n], bank[6 + r % 2][0:m, k * GT:k * GT + n])
                last.then_inc(sgt_done, 1)

            def take_ye(e):
                for c in range(2):
                    dve.wait_ge(f2_ps, 2 * e + c + 1)
                    bias = b2s[:, 2 * e + c:2 * e + c + 1]
                    full, m, w = (G - 1) * GB * CAP, GB * CAP, pics(G - 1) * CAP
                    nc.vector.tensor_scalar(
                        yeT[:, c, e // 4, 0:4 * full].rearrange("p (g e s) -> p g e s", g=G - 1, e=4)[:, :, e % 4, :],
                        bank[4 + c][:, 0:full].rearrange("p (g s) -> p g s", s=m), bias, None, ALU.add)
                    nc.vector.tensor_scalar(yeT[:, c, e // 4, 4 * full + e % 4 * w:4 * full + (e % 4 + 1) * w],
                                            bank[4 + c][:, full:SLOTS], bias, None, ALU.add).then_inc(ye_done, 1)

            def take_yq(q, g):
                i = q * G + g
                dve.wait_ge(yq_ps, i + 1)
                if i >= 6:
                    dve.wait_ge(sc_ps, i - 5)
                n = 4 * pics(g) * CAP
                nc.vector.tensor_copy(yq[0:n, i % 6, :], bank[yq_bank(q, g)][0:n, 0:D]).then_inc(yq_dve, 1)

            def add_out(q, g):
                n = rows(g)
                dve.wait_ge(sc_ps, q * G + g + 1)
                if q == 1:
                    dve.wait_ge(ob_done, g + 1)
                nc.vector.tensor_tensor(ob[0:n, g, :], bank[sc_bank(q, g)][0:n, 0:D],
                                        (h if q == 0 else ob)[0:n, g, :], ALU.add).then_inc(ob_done, 1)

            dve.wait_ge(in_b, 32)
            for e in range(E):
                if e == 4:
                    for g in range(G):
                        take_yq(0, g)
                        add_out(0, g)
                take_ye(e)
            for g in range(1, G, 2):
                take_yq(1, g)
            for g in range(G):
                add_out(1, g)

        @block.tensor
        def _(pe):
            def mm(out_, lhsT, rhs, start=True, stop=True, **kw):
                return nc.tensor.matmul(out_, lhsT, rhs, start=start, stop=stop, **kw)

            def transpose_rows(g, norm):
                n = rows(g)
                pe.wait_ge(xn_done, norm * G + g + 1)
                if norm == 0 and g == 0:
                    pe.wait_ge(in_const, 16)
                if g >= 2:
                    pe.wait_ge(xnt_done, norm * G + g - 1)
                for c in range(2):
                    last = mm(bank[2 + g % 2][:, c * n:c * n + n], xn[0:n, g, c * 128:c * 128 + 128],
                              ident[0:n, 0:n], is_transpose=True)
                last.then_inc(xnt_ps, 1)

            def project_qk(u):
                n = min(2 * GT, TOK - 2 * GT * u)
                t0 = 2 * GT * u
                pe.wait_ge(xnt_done, 2 * u + 2)
                if u == 0:
                    pe.wait_ge(in_bd, 16)
                if u >= 2:
                    pe.wait_ge(q_done, u - 1)
                    pe.wait_ge(k_done, u - 1)
                for which, done in ((0, q_ps), (1, k_ps)):
                    for c in range(2):
                        last = mm(bank[4 + 2 * (u % 2) + which][:, c * n:c * n + n], bds[:, which, :],
                                  xnT[:, c, t0:t0 + n])
                    last.then_inc(done, 1)

            pe.wait_ge(in_wl, 16)
            for g in range(G):
                n = rows(g)
                pe.wait_ge(in_xp[g], 16)
                if g >= 2:
                    pe.wait_ge(h_done, g - 1)
                x = xps[:, KF * GT * g:KF * GT * g + KF * n].rearrange("p (k t) -> p k t", k=KF)
                for k in range(KF):
                    last = mm(bank[g % 2][0:n, 0:D], x[:, k, :], wls[:, k, :], k == 0, k == KF - 1)
                last.then_inc(patch_done, 1)
                if g >= 2:
                    transpose_rows(g - 2, 0)
                if g == 3:
                    project_qk(0)
                if g == 5:
                    project_qk(1)
            transpose_rows(4, 0)
            transpose_rows(5, 0)
            project_qk(2)

            def values(p):
                pe.wait_ge(xn3_done, min(G, (2 * p + 1) // GB + 1))
                if p == 0:
                    pe.wait_ge(q_done, 2)
                else:
                    pe.wait_ge(vb_done, p)
                for b in range(2):
                    dst = bank[6][0:GT, b * D:b * D + D].rearrange("p (f c r) -> p c f r", f=2, c=2)
                    for c in range(2):
                        last = mm(dst[:, c, :, :], xn3[:, c, 2 * p + b, :], bds[:, 2, :])
                last.then_inc(v_ps, 1)

            def scores(p):
                s = 2 * (p % 2)
                if p == 0:
                    pe.wait_ge(constb_ready, 1)
                    pe.wait_ge(fills_done, 1)
                    pe.wait_ge(h_done, G)
                    pe.wait_ge(q_done, UNITS)
                    pe.wait_ge(km_done, 4 * UNITS)
                if p >= 2:
                    pe.wait_ge(sub_done, p - 1)
                for f in range(2):
                    for b in range(2):
                        mm(bank[s + f][64 * b:64 * b + 64, 0:8 * S], id64b[64 * f:64 * f + S, :],
                           causalb[64 * f:64 * f + S, :], True, False, skip_group_check=True)
                for c in range(2):
                    for f in range(2):
                        for b in range(2):
                            t = (2 * p + b) * S
                            last = mm(bank[s + f][64 * b:64 * b + 64, 4 * S * c:4 * S * (c + 1)],
                                      qT[64 * f:64 * f + 64, c, t:t + 64], km[64 * f:64 * f + 64, c, :, t:t + S],
                                      False, c == 1, skip_group_check=True)
                last.then_inc(s_ps, 1)

            def transpose_weights(p):
                pe.wait_ge(exp_done, p + 1)
                if p == 0:
                    pe.wait_ge(fills_done, 2)
                    pe.wait_ge(k_done, UNITS)
                else:
                    pe.wait_ge(pt_done, 2 * p)
                for t in range(TRIPLES):
                    last = mm(bank[4 + t // 4][0:GT, 128 * (t % 4):128 * (t % 4) + 128],
                              pr[:, p % 2, 3 * t:3 * t + 3, :], ident, is_transpose=True)
                last.then_inc(pt_ps, 1)

            def weigh_values(p):
                pe.wait_ge(pt_done, 2 * p + 2)
                pe.wait_ge(vb_done, p + 1)
                if p == 0:
                    pe.wait_ge(fills_done, 3)
                else:
                    pe.wait_ge(yt_done, p)
                for t in range(TRIPLES):
                    m = min(3, HEADS - 3 * t)
                    for b in range(2):
                        last = mm(bank[7][64 * b:64 * b + 64, 3 * t * VC:(3 * t + m) * VC],
                                  pT[0:GT, p % 2, t, 64 * b:64 * b + 64], vb[0:GT, p % 2, b, 3 * t:3 * t + m, :])
                last.then_inc(pv_ps, 1)

            def transpose_y(p):
                pe.wait_ge(y_done, p + 1)
                for c in range(2):
                    last = mm(bank[7][:, c * 128:c * 128 + 128], ys[:, p % 2, 8 * c:8 * c + 8, :], ident,
                              is_transpose=True)
                last.then_inc(yt_ps, 1)

            for p in range(PAIRS + 2):
                if p < PAIRS:
                    values(p)
                    scores(p)
                if p >= 2:
                    transpose_y(p - 2)
                if 1 <= p <= PAIRS:
                    transpose_weights(p - 1)
                    weigh_values(p - 1)

            def attention_out(g):
                n = rows(g)
                if g == 0:
                    pe.wait_ge(in_wu, 16)
                    pe.wait_ge(sub_done, PAIRS)
                pe.wait_ge(yt_done, min(PAIRS, (GB * (g + 1) + 1) // 2))
                if g >= 2:
                    pe.wait_ge(h_done, G + g - 1)
                for c in range(2):
                    last = mm(bank[g % 2][0:n, 0:D], yT[:, c, g * GT:g * GT + n], wus[:, c, :], c == 0, c == 1)
                last.then_inc(o_ps, 1)

            def route(g):
                pe.wait_ge(xnt_done, G + g + 1)
                if g == 0:
                    pe.wait_ge(in_rw, 16)
                if g == G - 1:
                    pe.wait_ge(fills_done, 5)
                for c in range(2):
                    last = mm(bank[4][0:GT, g * E:g * E + E], xnT[:, c, g * GT:g * GT + GT], rws[:, c, :], c == 0, c == 1)
                last.then_inc(logit_ps, 1)

            for g in range(G + 3):
                if g < G:
                    attention_out(g)
                if 2 <= g < G + 2:
                    transpose_rows(g - 2, 1)
                if g >= 3:
                    route(g - 3)

            pe.wait_ge(z_done, 1)
            for g in range(G):
                n = rows(g)
                last = mm(bank[5][:, 0:S], zr[0:n, g, :], const[0:n, C_D38:C_D38 + S], g == 0, g == G - 1)
            last.then_inc(route_ps, 1)
            pe.wait_ge(lall_done, 1)
            for g in range(G):
                last = mm(bank[6][0:GT, g * E:g * E + E], lall[:, GB * g:GB * g + GB, :], e8b)
            last.then_inc(slot_ps, 1)
            pe.wait_ge(h_done, 2 * G)
            for g in range(G):
                n, m = rows(g), pics(g) * CAP
                pe.wait_ge(sel_done, g + 1)
                if g >= 4:
                    pe.wait_ge(gather_act if g % 2 == 0 else gather_dve, (g - 4) // 2 + 1)
                for c in range(2):
                    last = mm(bank[g % 4][:, c * E * m:c * E * m + E * m], xn[0:n, g, c * 128:c * 128 + 128],
                              sel[0:n, g, 0:E * m])
                last.then_inc(gather_ps, 1)

            def layer1(e):
                pe.wait_ge(in_w1[e % NBUF], 16 * (e // NBUF + 1))
                if e == 0:
                    pe.wait_ge(gather_act, G // 2)
                    pe.wait_ge(gather_dve, G // 2)
                for c in range(NH):
                    i = e * NH + c
                    if i >= 4:
                        pe.wait_ge(gelu_done, i - 3)
                    for k in range(2):
                        last = mm(bank[i % 4][:, 0:SLOTS], w1s[:, e % NBUF, k, c * 128:c * 128 + 128], tokT[:, k, e, :],
                                  k == 0, k == 1)
                    last.then_inc(f1_ps, 1)

            def layer2(e):
                pe.wait_ge(in_w2[e % NBUF], 16 * (e // NBUF + 1))
                pe.wait_ge(gelu_done, NH * (e + 1))
                for c in range(2):
                    if e >= 1:
                        pe.wait_ge(ye_done, 2 * e - 1 + c)
                    for k in range(NH):
                        last = mm(bank[4 + c][:, 0:SLOTS], w2s[:, e % NBUF, k, c * 128:c * 128 + 128],
                                  gT[:, e % 2, k, :], k == 0, k == NH - 1)
                    last.then_inc(f2_ps, 1)

            def transpose_gates(r):
                if r >= 2:
                    pe.wait_ge(sgt_done, r - 1)
                for k in range(4):
                    q, g = divmod(4 * r + k, G)
                    n, m = rows(g), pics(g) * CAP
                    pe.wait_ge(selg_done, g + 1)
                    last = mm(bank[6 + r % 2][0:4 * m, k * GT:k * GT + n], selg[0:n, g, 4 * q * m:4 * (q + 1) * m],
                              ident[0:n, 0:n], is_transpose=True)
                last.then_inc(sgt_ps, 1)

            def transpose_ye(q, g):
                m = pics(g) * CAP
                if q == 0 and g >= 1:
                    pe.wait_ge(yq_dve, g)
                if q == 1 and g < 4:
                    pe.wait_ge(gelu_done, NH * E)
                if q == 1 and g >= 4:
                    pe.wait_ge(yq_act if g % 2 == 0 else yq_dve, (g - 4) // 2 + 1 + (0 if g % 2 == 0 else G))
                for c in range(2):
                    last = mm(bank[yq_bank(q, g)][0:4 * m, c * 128:c * 128 + 128],
                              yeT[:, c, q, 4 * g * GB * CAP:4 * g * GB * CAP + 4 * m], ident, is_transpose=True)
                last.then_inc(yq_ps, 1)

            def scatter(q, g):
                n, m = rows(g), 4 * pics(g) * CAP
                if q == 0:
                    pe.wait_ge(yq_dve, g + 1)
                    if g >= 1:
                        pe.wait_ge(ob_done, g)
                else:
                    pe.wait_ge(yq_act if g % 2 == 0 else yq_dve, g // 2 + 1 + (0 if g % 2 == 0 else G))
                    pe.wait_ge(ob_done, G + max(0, g - 1))
                mm(bank[sc_bank(q, g)][0:n, 0:D], sgT[0:m, q, g, 0:n], yq[0:m, (q * G + g) % 6, :]).then_inc(sc_ps, 1)

            layer1(0)
            for r in range(3):
                transpose_gates(r)
            for e in range(E):
                if e + 1 < E:
                    layer1(e + 1)
                if e == 4:
                    pe.wait_ge(sgt_done, 3)
                    pe.wait_ge(ye_done, 8)
                    for g in range(G):
                        transpose_ye(0, g)
                        scatter(0, g)
                layer2(e)
            pe.wait_ge(ye_done, 2 * E)
            for g in range(G):
                transpose_ye(1, g)
            for g in range(G):
                scatter(1, g)


def shape_constants():
    import numpy as np
    c = np.zeros((128, C_END), np.float32)
    p = np.arange(128)
    c[:, C_ID:C_ID + 128] = np.eye(128)
    for m in range(4):
        c[:, C_KM + m] = 0.25 * ((p % 64) // HC == m)
    for i in range(HEADS):
        c[:, C_M3 + i] = p // S == i % 3
    for b in range(GB):
        for s in range(CAP):
            c[:, C_PAT + b * CAP + s] = np.where(p // S == b, s + 1, -1)
        c[:, C_ZM + b] = p // S == b
    for s in range(S):
        c[:, C_D38 + s] = p % S == s
    for b in range(G * GB):
        c[:, C_LM + b] = p // E == b
    for e in range(E):
        c[:, C_E8 + e] = p % E == e
    for r in (0, 64):
        for i in range(S):
            c[r + i, C_I64 + i] = 1
    for r in (0, 64):
        for i in range(S):
            for hd in range(8):
                c[r + i, C_CM + hd * S + i + 1:C_CM + hd * S + S] = MASKED
    return c


def kernel(x, cls_tok, L0_tok_W_lin, L0_tok_b_lin, L0_tok_class_token, L0_tok_position_embeddings, L0_attn_Wq,
           L0_attn_Wk, L0_attn_Wv, L0_attn_Wu, L0_attn_bu, L0_ffn_router_w, L0_ffn_w1, L0_ffn_b1, L0_ffn_w2,
           L0_ffn_b2):
    import numpy as np
    import concourse.bacc as bacc
    from concourse.bass_utils import run_bass_kernel_spmd

    a = lambda v: np.ascontiguousarray(np.asarray(v))
    side = IMG // PATCH
    xf = a(x).reshape(B, C_IN, side, PATCH, side, PATCH).transpose(1, 3, 5, 0, 2, 4).reshape(F, B, NPATCH)
    xt = np.zeros((F, B, S), np.float32)
    xt[:, :, 2:] = xf
    xt = xt.reshape(KF, 128, TOK)
    xp = np.concatenate([xt[:, :, g * GT:g * GT + rows(g)].transpose(1, 0, 2).reshape(128, -1) for g in range(G)], axis=1)
    wl = a(L0_tok_W_lin).T.reshape(KF, 128, D).transpose(1, 0, 2)
    one_a = np.concatenate([a(cls_tok).reshape(1, D), a(L0_tok_position_embeddings).reshape(S - 1, D)])
    one_b = np.concatenate([np.zeros((1, D), np.float32), a(L0_tok_class_token).reshape(1, D),
                            np.repeat(a(L0_tok_b_lin).reshape(1, D), NPATCH, axis=0)])
    rows_a, rows_b = (np.resize(v, (128, D)) for v in (one_a, one_b))
    bd = np.zeros((128, 3, 128), np.float32)
    for w, m in enumerate((L0_attn_Wq, L0_attn_Wk, L0_attn_Wv)):
        for i in range(128 // HC):
            bd[i * HC:(i + 1) * HC, w, i * HC:(i + 1) * HC] = a(m).T
    wu = a(L0_attn_Wu).T.reshape(2, 128, D).transpose(1, 0, 2)
    bu = np.repeat(a(L0_attn_bu).reshape(1, D), 128, axis=0)
    rw = a(L0_ffn_router_w).T.reshape(2, 128, E).transpose(1, 0, 2)
    w1 = a(L0_ffn_w1).reshape(E, 2, 128, HID).transpose(0, 2, 1, 3)
    b1 = a(L0_ffn_b1).reshape(E * NH, 128).T
    w2 = a(L0_ffn_w2).reshape(E, NH, 128, D).transpose(0, 2, 1, 3)
    b2 = a(L0_ffn_b2).reshape(E * 2, 128).T
    arrays = dict(xp=xp, wl=wl, rows_a=rows_a, rows_b=rows_b, bd=bd, wu=wu, bu=bu, rw=rw, w1=w1, b1=b1, w2=w2, b2=b2,
                  consts=shape_constants())
    arrays = {f"{n}_dram": np.ascontiguousarray(v) for n, v in arrays.items()}

    nc = bacc.Bacc("TRN2", target_bir_lowering=False, num_devices=1)
    args = [nc.dram_tensor(n, v.shape, mybir.dt.float32, kind="ExternalInput").ap() for n, v in arrays.items()]
    out = nc.dram_tensor("out_dram", (TOK, D), mybir.dt.float32, kind="ExternalOutput").ap()
    tower(nc, *args, out)
    r = run_bass_kernel_spmd(nc, [arrays], core_ids=[0])
    return r.results[0]["out_dram"].reshape(B, S, D)
```

```python
from contextlib import ExitStack

import concourse.bass as bass
from concourse import mybir

B, C_IN, IMG, PATCH = 16, 3, 96, 16
D, HEADS, HC = 256, 16, 16
NPATCH = (IMG // PATCH) ** 2
S = NPATCH + 2
TOK = B * S
F = C_IN * PATCH * PATCH
KF = F // 128
E, HID = 8, 1024
NH = HID // 128
CAP = max(1, int(S * 2.0 / E) + 1)
SLOTS = B * CAP

GB = 3
GT = GB * S
G = -(-B // GB)
GTP = G * GT
PAIRS = B // 2
UNITS = G // 2
QW = 64
POS = 18
TRIPLES = POS // 3
VC = HC + 1
NBUF = 4
MASKED = -1e30
SETS = ((0, 4), (4, G))
SET_ROWS = [(min(b * GB, B) - a * GB) * E for a, b in SETS]
SLOTS_A = SETS[0][1] * GB * CAP

C_ID, C_KM, C_M3, C_PAT, C_ZM, C_D38, C_LM, C_E8, C_I64 = 0, 128, 132, 148, 178, 181, 219, 231, 239
C_CM = C_I64 + 64
C_END = C_CM + 8 * S


def rows(g):
    return min(GT, TOK - g * GT)


def pics(g):
    return min(GB, B - g * GB)


def unit_rows(u):
    return min(2 * GT, TOK - 2 * GT * u)


def pair_needs(g):
    return min(PAIRS, (GB * (g + 1) + 1) // 2)


def tower(nc, xp, wl, rows_a, rows_b, bd, wu, bu, rw, w1, b1, w2, b2, consts, out):
    fp32, bf16 = mybir.dt.float32, mybir.dt.bfloat16
    ALU, ACT, AX = mybir.AluOpType, mybir.ActivationFunctionType, mybir.AxisListType

    with ExitStack() as ctx:
        def sb(name, shape, dt=fp32):
            return ctx.enter_context(nc.sbuf_tensor(name, shape, dt))

        def sem(name):
            return ctx.enter_context(nc.semaphore(name))

        const = sb("const", [128, C_END])
        ident = const[:, C_ID:C_ID + 128]
        constb = sb("constb", [128, C_END - C_E8], bf16)
        e8b = constb[:, 0:8]
        id64b = constb[:, C_I64 - C_E8:C_I64 - C_E8 + 64]
        causalb = constb[:, C_CM - C_E8:C_CM - C_E8 + 8 * S]
        xps = sb("xps", [128, KF * TOK])
        wls = sb("wls", [128, KF, D])
        add_a = sb("add_a", [128, D])
        add_b = sb("add_b", [128, D])
        bds = sb("bds", [128, 3, 128])
        wus = sb("wus", [128, 2, D])
        bus = sb("bus", [128, D])
        rws = sb("rws", [128, 2, E])
        b1s = sb("b1s", [128, E * NH])
        b2s = sb("b2s", [128, E * 2])
        w1s = sb("w1s", [128, NBUF, 2, HID])
        w2s = sb("w2s", [128, NBUF, NH, D])
        h = sb("h", [128, G, D])
        hb = sb("hb", [128, G, D])
        xn = sb("xn", [128, G, D])
        stat = sb("stat", [128, G, 6])
        mv = sb("mv", [128, G, 2])
        ve = sb("ve", [128, G])
        lnv = sb("lnv", [128, G])
        r0 = sb("r0", [128, G])
        nt = sb("nt", [128, G, 2])
        rstd = sb("rstd", [128, G])
        xnT = sb("xnT", [128, 2, GTP])
        qT = sb("qT", [128, 2, B, QW])
        kf = sb("kf", [128, 2, 2, 2 * GT])
        km = sb("km", [128, 2, 4, TOK])
        vb = sb("vb", [128, 2, 2, HEADS, VC])
        mx = sb("mx", [128, 2, HEADS])
        pr = sb("pr", [128, 2, POS, S])
        pT = sb("pT", [128, 2, TRIPLES, 128])
        rs = sb("rs", [128, 2, HEADS])
        ys = sb("ys", [128, 2, HEADS, HC])
        yT = sb("yT", [128, 2, TOK])
        rmax = sb("rmax", [128, G])
        lsh = sb("lsh", [128, G, E])
        lex = sb("lex", [128, G, E])
        rsum = sb("rsum", [128, G])
        rrec = sb("rrec", [128, G])
        sc = sb("sc", [128, G, E])
        zr = sb("zr", [128, G, SET_ROWS[0]])
        rv = sb("rv", [128, 2, S])
        rv2 = sb("rv2", [128, 2, S])
        top = sb("top", [128, 2, 2, 8])
        isgt = sb("isgt", [128, 2, S])
        ngt = sb("ngt", [128, 2])
        iseq = sb("iseq", [128, 2, S])
        ceq = sb("ceq", [128, 2, S])
        fits = sb("fits", [128, 2, S])
        picked = sb("picked", [128, 2, S])
        cpick = sb("cpick", [128, 2, S])
        slot = sb("slot", [128, 2, S])
        lall = sb("lall", [128, G * GB, S], bf16)
        shared = sb("shared", [128, 2 * B * GT])
        xn3 = shared[:, :].rearrange("p (c b r) -> p c b r", c=2, b=B)
        sel = shared[:, 0:G * E * GB * CAP].rearrange("p (g s) -> p g s", g=G)
        selg = shared[:, G * E * GB * CAP:2 * G * E * GB * CAP].rearrange("p (g s) -> p g s", g=G)
        tokT = sb("tokT", [128, 2, E, SLOTS])
        gT = km[:].rearrange("p c m t -> p (c m t)")[:, 0:2 * NH * SLOTS].rearrange("p (b k s) -> p b k s", b=2, k=NH)
        yeT = xps[:, 0:2 * E * SLOTS].rearrange("p (c q s) -> p c q s", c=2, q=2)
        sgT = pT[:].rearrange("p b t n -> p (b t n)")[:, 0:2 * G * GT].rearrange("p (q g t) -> p q g t", q=2, g=G)
        yq = wls
        ob = hb

        bank = [ctx.enter_context(nc.psum_tensor(f"bank{i}", [128, 512], fp32)) for i in range(8)]
        S_BANK, V_BANK, P_BANK, Y_BANK = (0, 1), 2, (3, 4), 5
        PATCH_BANK = (6, 7, 6, 7, 6, 7)
        T_BANK = ((2, 3, 4, 5, 6, 7), (7, 7, 7, 7, 6, 7))
        Q_BANK, K_BANK = (0, 6, 6), (1, 7, 7)
        O_BANK = (6, 6, 6, 6, 6, 7)
        LOGIT_BANK, LOGIT_COL = (7, 5), 256
        ROUTE_BANK = 2
        GATHER_BANK = (0, 1, 3, 4, 2, 5)
        F1_BANK, F2_BANK = (0, 1, 3, 4), (2, 5)
        GATE_BANK = (6, 7, 6)
        YQ_BANK = ((6,) * G, (0, 1, 3, 4, 6, 7))
        SC_BANK = ((7,) * G, (2, 5, 0, 1, 2, 5))

        in_const, in_rows, in_bd, in_wu, in_bu, in_rw, in_b = (
            sem(n) for n in ("in_const", "in_rows", "in_bd", "in_wu", "in_bu", "in_rw", "in_b"))
        in_wl = [sem(f"in_wl{i}") for i in range(3)]
        in_xp = [sem(f"in_xp{g}") for g in range(G)]
        in_w1 = [sem(f"in_w1_{i}") for i in range(NBUF)]
        in_w2 = [sem(f"in_w2_{i}") for i in range(NBUF)]
        (constb_ready, rows_ready, qpad_ready, empty_heads_ready, xnT_pad_ready, ones_ready, zr_ready, hb_done,
         selg_done) = (
            sem(n) for n in ("constb_ready", "rows_ready", "qpad_ready", "empty_heads_ready", "xnT_pad_ready",
                             "ones_ready", "zr_ready", "hb_done", "selg_done"))
        (patch_done, xnt_ps, q_ps, k_ps, v_ps, s_ps, pt_ps, pv_ps, yt_ps, o_ps, logit_ps, route_ps, slot_ps,
         gather_ps, sgt_ps, f1_ps, f2_ps, yq_ps, sc_ps) = (
            sem(n) for n in ("patch_done", "xnt_ps", "q_ps", "k_ps", "v_ps", "s_ps", "pt_ps", "pv_ps", "yt_ps",
                             "o_ps", "logit_ps", "route_ps", "slot_ps", "gather_ps", "sgt_ps", "f1_ps", "f2_ps",
                             "yq_ps", "sc_ps"))
        (h_done, stats_done, mv_done, ve_done, nt_done, rstd_done, xn_done, km_done, vb_done, mx_done, sub_done,
         rs_done, y_done, soft_done, lsh_done, sc_done, z_done, topk_done, lall_done, sel_done, sgt_done, ye_done,
         ob_done, gather_dve, yq_dve) = (
            sem(n) for n in ("h_done", "stats_done", "mv_done", "ve_done", "nt_done", "rstd_done", "xn_done",
                             "km_done", "vb_done", "mx_done", "sub_done", "rs_done", "y_done", "soft_done",
                             "lsh_done", "sc_done", "z_done", "topk_done", "lall_done", "sel_done", "sgt_done",
                             "ye_done", "ob_done", "gather_dve", "yq_dve"))
        (ln_done, r0_done, xnt_done, q_done, k_done, exp_done, pt_done, yt_done, lex_done, gather_act,
         gelu_done, yq_act) = (
            sem(n) for n in ("ln_done", "r0_done", "xnt_done", "q_done", "k_done", "exp_done", "pt_done", "yt_done",
                             "lex_done", "gather_act", "gelu_done", "yq_act"))
        stored = sem("stored")

        def f1_count(e):
            return NH * (e + 2)

        block = ctx.enter_context(nc.Block())

        @block.sync
        def _(sp):
            for i in range(3):
                sp.dma_start(wls[:, 2 * i:2 * i + 2, :], wl[:, 2 * i:2 * i + 2, :]).then_inc(in_wl[i], 16)
            for g in range(1, G):
                a = KF * GT * g
                sp.dma_start(xps[:, a:a + KF * rows(g)], xp[:, a:a + KF * rows(g)]).then_inc(in_xp[g], 16)
            sp.dma_start(wus[:], wu).then_inc(in_wu, 16)
            sp.dma_start(rws[:], rw).then_inc(in_rw, 16)
            sp.dma_start(b1s[:], b1).then_inc(in_b, 16)
            sp.dma_start(b2s[:], b2).then_inc(in_b, 16)
            for e in range(E):
                if e >= NBUF:
                    sp.wait_ge(f1_ps, f1_count(e - NBUF))
                sp.dma_start(w1s[:, e % NBUF, :, :], w1[e, :, :, :]).then_inc(in_w1[e % NBUF], 16)
                if e >= NBUF:
                    sp.wait_ge(f2_ps, 2 * (e - NBUF + 1))
                sp.dma_start(w2s[:, e % NBUF, :, :], w2[e, :, :, :]).then_inc(in_w2[e % NBUF], 16)
            for g in range(G):
                sp.wait_ge(ob_done, G + g + 1)
                sp.dma_start(out[g * GT:g * GT + rows(g), :], ob[0:rows(g), g, :]).then_inc(stored, 16)
            sp.wait_ge(stored, 16 * G)

        @block.gpsimd
        def _(pool):
            nc.gpsimd.memset(qT[:, :, :, S:QW], 0.0).then_inc(qpad_ready, 1)
            nc.gpsimd.memset(pr[:, :, HEADS:POS, :], 0.0).then_inc(empty_heads_ready, 1)
            nc.gpsimd.memset(xnT[:, :, TOK:GTP], 0.0).then_inc(xnT_pad_ready, 1)
            pool.wait_ge(in_rows, 32)
            nc.gpsimd.tensor_tensor(add_a[:], add_a[:], add_b[:], ALU.add).then_inc(rows_ready, 1)
            pool.wait_ge(in_const, 16)
            nc.gpsimd.tensor_copy(constb[:], const[:, C_E8:C_END]).then_inc(constb_ready, 1)
            nc.gpsimd.tensor_copy(
                vb[:, :, :, :, HC], const[:, C_M3:C_M3 + HEADS].unsqueeze(1).unsqueeze(1).to_broadcast([128, 2, 2, HEADS])
            ).then_inc(ones_ready, 1)
            nc.gpsimd.memset(zr[:], 0.0).then_inc(zr_ready, 1)
            pool.wait_ge(in_bu, 16)
            for g in range(G):
                pool.wait_ge(h_done, g + 1)
                nc.gpsimd.tensor_tensor(hb[0:rows(g), g, :], h[0:rows(g), g, :], bus[0:rows(g), :],
                                        ALU.add).then_inc(hb_done, 1)
            for g in range(G):
                pool.wait_ge(sel_done, g + 1)
                n = pics(g) * CAP
                nc.gpsimd.tensor_tensor(
                    selg[0:rows(g), g, 0:E * n].rearrange("p (e s) -> p e s", e=E),
                    sel[0:rows(g), g, 0:E * n].rearrange("p (e s) -> p e s", e=E),
                    sc[0:rows(g), g, :].unsqueeze(2).to_broadcast([rows(g), E, n]), ALU.mult).then_inc(selg_done, 1)

        @block.scalar
        def _(act):
            act.dma_start(xps[:, 0:KF * rows(0)], xp[:, 0:KF * rows(0)]).then_inc(in_xp[0], 16)
            act.dma_start(add_a[:], rows_a).then_inc(in_rows, 16)
            act.dma_start(add_b[:], rows_b).then_inc(in_rows, 16)
            act.dma_start(const[:], consts).then_inc(in_const, 16)
            act.dma_start(bds[:], bd).then_inc(in_bd, 16)
            act.dma_start(bus[:], bu).then_inc(in_bu, 16)
            nc.scalar.preload_act_table_set("natural_log_exp_and_others")

            def first_rstd(g, norm):
                n = rows(g)
                act.wait_ge(ve_done, norm * G + g + 1)
                nc.scalar.activation(lnv[0:n, g:g + 1], ve[0:n, g:g + 1], ACT.Ln).then_inc(ln_done, 1)
                act.wait_ge(ln_done, norm * G + g + 1)
                nc.scalar.activation(r0[0:n, g:g + 1], lnv[0:n, g:g + 1], ACT.Exp, scale=-0.5).then_inc(r0_done, 1)

            def take_xnT(g, norm):
                n, m = rows(g), pics(g)
                act.wait_ge(xnt_ps, norm * G + g + 1)
                src = bank[T_BANK[norm][g]][:, 0:2 * n].rearrange("p (c t) -> p c t", c=2)
                if norm == 0:
                    for c in range(2):
                        nc.scalar.activation(
                            xn3[:, c, g * GB:g * GB + m, :].rearrange("p b (r t) -> p b r t", r=3),
                            src[:, c, :].rearrange("p (b t) -> p b t", t=S).unsqueeze(2).to_broadcast([128, m, 3, S]),
                            ACT.Copy)
                nc.scalar.activation(xnT[:, :, g * GT:g * GT + n], src, ACT.Copy).then_inc(xnt_done, 1)

            def take_qk(u):
                n = unit_rows(u)
                b0 = 2 * GB * u
                if u == 0:
                    act.wait_ge(qpad_ready, 1)
                act.wait_ge(q_ps, u + 1)
                nc.scalar.activation(qT[:, :, b0:b0 + n // S, 0:S],
                                     bank[Q_BANK[u]][:, 0:2 * n].rearrange("p (c b t) -> p c b t", c=2, t=S),
                                     ACT.Copy, scale=0.25).then_inc(q_done, 1)
                act.wait_ge(k_ps, u + 1)
                if u >= 2:
                    act.wait_ge(km_done, 4 * (u - 1))
                nc.scalar.activation(kf[:, u % 2, :, 0:n],
                                     bank[K_BANK[u]][:, 0:2 * n].rearrange("p (c t) -> p c t", c=2),
                                     ACT.Copy).then_inc(k_done, 1)

            def take_pT(p):
                act.wait_ge(pt_ps, p + 1)
                if p >= 2:
                    act.wait_ge(pv_ps, p - 1)
                nc.scalar.activation(pT[0:GT, p % 2, 0:4, :],
                                     bank[P_BANK[0]][0:GT, :].rearrange("p (t n) -> p t n", t=4),
                                     ACT.Copy).then_inc(pt_done, 1)
                nc.scalar.activation(pT[0:GT, p % 2, 4:6, :],
                                     bank[P_BANK[1]][0:GT, 0:256].rearrange("p (t n) -> p t n", t=2),
                                     ACT.Copy).then_inc(pt_done, 1)

            def take_yT(p):
                act.wait_ge(yt_ps, p + 1)
                nc.scalar.activation(
                    yT[:, :, 2 * p * S:2 * (p + 1) * S].rearrange("p c (b t) -> p c b t", b=2),
                    bank[Y_BANK][:, 0:256].rearrange("p (c b t) -> p c b t", c=2, b=2)[:, :, :, 0:S],
                    ACT.Copy).then_inc(yt_done, 1)

            def weights(p):
                act.wait_ge(sub_done, p + 1)
                nc.scalar.activation(pr[:, p % 2, 0:HEADS, :], pr[:, p % 2, 0:HEADS, :], ACT.Exp).then_inc(exp_done, 1)

            def router_exp(k):
                a, b = SETS[k]
                act.wait_ge(lsh_done, k + 1)
                nc.scalar.activation(lex[0:GT, a:b, :], lsh[0:GT, a:b, :], ACT.Exp).then_inc(lex_done, 1)

            def take_tokens(g):
                act.wait_ge(gather_ps, g + 1)
                n = pics(g) * CAP
                nc.scalar.activation(tokT[:, :, :, g * GB * CAP:g * GB * CAP + n],
                                     bank[GATHER_BANK[g]][:, 0:2 * E * n].rearrange("p (c e s) -> p c e s", c=2, e=E),
                                     ACT.Copy).then_inc(gather_act, 1)

            first_rstd(0, 0)
            first_rstd(1, 0)
            first_rstd(2, 0)
            take_xnT(0, 0)
            take_xnT(1, 0)
            first_rstd(3, 0)
            take_xnT(2, 0)
            take_qk(0)
            first_rstd(4, 0)
            take_xnT(3, 0)
            first_rstd(5, 0)
            weights(0)
            take_qk(1)
            take_pT(0)
            weights(1)
            take_xnT(4, 0)
            take_yT(0)
            take_pT(1)
            take_xnT(5, 0)
            weights(2)
            take_qk(2)
            take_yT(1)
            take_pT(2)
            for p in range(3, 7):
                if p >= 4:
                    first_rstd(p - 4, 1)
                weights(p)
                take_yT(p - 1)
                take_pT(p)
                if p >= 4:
                    take_xnT(p - 4, 1)
            first_rstd(3, 1)
            weights(7)
            take_xnT(3, 1)
            take_pT(7)
            take_yT(6)
            router_exp(0)
            take_yT(7)
            first_rstd(4, 1)
            first_rstd(5, 1)
            take_tokens(0)
            take_xnT(4, 1)
            take_xnT(5, 1)
            router_exp(1)
            take_tokens(2)

            act.wait_ge(in_b, 32)
            i = 0
            for e in range(E):
                if e >= 2:
                    act.wait_ge(f2_ps, 2 * (e - 1))
                for a, b in ((0, SLOTS_A), (SLOTS_A, SLOTS)) if e == 0 else ((0, SLOTS),):
                    if a:
                        take_tokens(4)
                    for c in range(NH):
                        act.wait_ge(f1_ps, i + 1)
                        nc.scalar.activation(gT[:, e % 2, c, a:b], bank[F1_BANK[i % 4]][:, 0:b - a], ACT.Gelu,
                                             bias=b1s[:, e * NH + c:e * NH + c + 1]).then_inc(gelu_done, 1)
                        i += 1
            for g in range(G):
                act.wait_ge(yq_ps, G + g + 1)
                act.wait_ge(sc_ps, g + 1)
                n = 4 * pics(g) * CAP
                nc.scalar.activation(yq[0:n, g, :], bank[YQ_BANK[1][g]][0:n, 0:D], ACT.Copy).then_inc(yq_act, 1)

        @block.vector
        def _(dve):
            def norm_stats(g, norm):
                n = rows(g)
                k = norm * G + g + 1
                if norm == 0:
                    dve.wait_ge(patch_done, g + 1)
                    dve.wait_ge(rows_ready, 1)
                    nc.vector.tensor_tensor(h[0:n, g, :], bank[PATCH_BANK[g]][0:n, 0:D], add_a[0:n, :],
                                            ALU.add).then_inc(h_done, 1)
                else:
                    dve.wait_ge(o_ps, g + 1)
                    dve.wait_ge(hb_done, g + 1)
                    nc.vector.tensor_tensor(h[0:n, g, :], bank[O_BANK[g]][0:n, 0:D], hb[0:n, g, :],
                                            ALU.add).then_inc(h_done, 1)
                dve.wait_ge(h_done, k)
                nc.vector.bn_stats(stat[0:n, g, :], h[0:n, g, :]).then_inc(stats_done, 1)
                dve.wait_ge(stats_done, k)
                nc.vector.bn_aggr(mv[0:n, g, :], stat[0:n, g, :]).then_inc(mv_done, 1)
                dve.wait_ge(mv_done, k)
                nc.vector.tensor_scalar(ve[0:n, g:g + 1], mv[0:n, g, 1:2], 1e-5, None, ALU.add).then_inc(ve_done, 1)

            def norm_apply(g, norm):
                n = rows(g)
                k = norm * G + g + 1
                dve.wait_ge(r0_done, k)
                nc.vector.scalar_tensor_tensor(nt[0:n, g, 0:1], r0[0:n, g:g + 1], ve[0:n, g:g + 1], r0[0:n, g:g + 1],
                                               ALU.mult, ALU.mult).then_inc(nt_done, 1)
                dve.wait_ge(nt_done, 2 * k - 1)
                nc.vector.tensor_scalar(nt[0:n, g, 1:2], nt[0:n, g, 0:1], -0.5, 1.5, ALU.mult, ALU.add).then_inc(nt_done, 1)
                dve.wait_ge(nt_done, 2 * k)
                nc.vector.tensor_tensor(rstd[0:n, g:g + 1], r0[0:n, g:g + 1], nt[0:n, g, 1:2], ALU.mult).then_inc(rstd_done, 1)
                dve.wait_ge(rstd_done, k)
                if norm == 1:
                    dve.wait_ge(xnt_ps, G)
                dst, src = xn[0:n, g, :], h[0:n, g, :]
                if norm == 0:
                    dst = dst.rearrange("p (c f r) -> p c f r", c=2, f=2)
                    src = src.rearrange("p (f c r) -> p c f r", c=2, f=2)
                nc.vector.tensor_scalar(dst, src, mv[0:n, g, 0:1], rstd[0:n, g:g + 1],
                                        ALU.subtract, ALU.mult).then_inc(xn_done, 1)

            def spread_k(u):
                n = unit_rows(u)
                t0 = 2 * GT * u
                dve.wait_ge(k_done, u + 1)
                for m in range(4):
                    nc.vector.tensor_scalar(km[:, :, m, t0:t0 + n], kf[:, u % 2, :, 0:n],
                                            const[:, C_KM + m:C_KM + m + 1], None, ALU.mult).then_inc(km_done, 1)

            def subtract_max(p):
                dve.wait_ge(s_ps, p + 1)
                for f in range(2):
                    nc.vector.tensor_reduce(mx[:, p % 2, 8 * f:8 * f + 8],
                                            bank[S_BANK[f]][:, 0:8 * S].rearrange("p (h t) -> p h t", h=8), AX.X,
                                            ALU.max).then_inc(mx_done, 1)
                if p >= 2:
                    dve.wait_ge(pt_ps, p - 1)
                for f in range(2):
                    dve.wait_ge(mx_done, 2 * p + f + 1)
                    last = nc.vector.tensor_tensor(
                        pr[:, p % 2, 8 * f:8 * f + 8, :],
                        bank[S_BANK[f]][:, 0:8 * S].rearrange("p (h t) -> p h t", h=8),
                        mx[:, p % 2, 8 * f:8 * f + 8].unsqueeze(2).to_broadcast([128, 8, S]), ALU.subtract)
                last.then_inc(sub_done, 1)

            def take_v(p):
                dve.wait_ge(v_ps, p + 1)
                if p >= 2:
                    dve.wait_ge(pv_ps, p - 1)
                nc.vector.tensor_tensor(
                    vb[0:GT, p % 2, :, :, 0:HC], bank[V_BANK][0:GT, :].rearrange("p (b h c) -> p b h c", b=2, h=HEADS),
                    const[0:GT, C_M3:C_M3 + HEADS].unsqueeze(1).unsqueeze(3).to_broadcast([GT, 2, HEADS, HC]),
                    ALU.mult).then_inc(vb_done, 1)

            def divide(p):
                y = bank[Y_BANK][:, 0:HEADS * VC].rearrange("p (h c) -> p h c", h=HEADS)
                dve.wait_ge(pv_ps, p + 1)
                nc.vector.reciprocal(rs[:, p % 2, :], y[:, :, HC]).then_inc(rs_done, 1)
                dve.wait_ge(rs_done, p + 1)
                if p >= 2:
                    dve.wait_ge(yt_ps, p - 1)
                nc.vector.tensor_tensor(ys[:, p % 2, :, :], y[:, :, 0:HC],
                                        rs[:, p % 2, :].unsqueeze(2).to_broadcast([128, HEADS, HC]),
                                        ALU.mult).then_inc(y_done, 1)

            def router_softmax(k):
                a, b = SETS[k]
                w = b - a
                logits = bank[LOGIT_BANK[k]][0:GT, LOGIT_COL:LOGIT_COL + w * E].rearrange("p (g e) -> p g e", e=E)
                dve.wait_ge(logit_ps, b)
                nc.vector.tensor_reduce(rmax[0:GT, a:b], logits, AX.X, ALU.max).then_inc(soft_done, 1)
                dve.wait_ge(soft_done, 3 * k + 1)
                nc.vector.tensor_tensor(lsh[0:GT, a:b, :], logits, rmax[0:GT, a:b].unsqueeze(2).to_broadcast([GT, w, E]),
                                        ALU.subtract).then_inc(lsh_done, 1)
                dve.wait_ge(lex_done, k + 1)
                nc.vector.tensor_reduce(rsum[0:GT, a:b], lex[0:GT, a:b, :], AX.X, ALU.add).then_inc(soft_done, 1)
                dve.wait_ge(soft_done, 3 * k + 2)
                nc.vector.reciprocal(rrec[0:GT, a:b], rsum[0:GT, a:b]).then_inc(soft_done, 1)
                dve.wait_ge(soft_done, 3 * k + 3)
                nc.vector.tensor_tensor(sc[0:GT, a:b, :], lex[0:GT, a:b, :],
                                        rrec[0:GT, a:b].unsqueeze(2).to_broadcast([GT, w, E]),
                                        ALU.mult).then_inc(sc_done, 1)
                dve.wait_ge(sc_done, k + 1)
                if k == 0:
                    dve.wait_ge(zr_ready, 1)
                for g in range(a, b):
                    n, m, c0 = rows(g), pics(g), (g - a) * GB * E
                    last = nc.vector.tensor_tensor(
                        zr[0:n, g, c0:c0 + m * E].rearrange("p (b e) -> p b e", b=m),
                        sc[0:n, g, :].unsqueeze(1).to_broadcast([n, m, E]),
                        const[0:n, C_ZM:C_ZM + m].unsqueeze(2).to_broadcast([n, m, E]), ALU.mult)
                last.then_inc(z_done, 1)

            steps = [0]

            def step(ins):
                ins.then_inc(topk_done, 1)
                steps[0] += 1
                dve.wait_ge(topk_done, steps[0])

            def best_tokens(k):
                r = slice(0, SET_ROWS[k])
                dve.wait_ge(route_ps, k + 1)
                step(nc.vector.tensor_copy(rv[r, k, :], bank[ROUTE_BANK][r, 0:S]))
                step(nc.vector.max(top[r, k, 0, :], rv[r, k, :]))
                step(nc.vector.match_replace(rv2[r, k, :], top[r, k, 0, :], rv[r, k, :], -1.0))
                step(nc.vector.max(top[r, k, 1, :], rv2[r, k, :]))

            def number_slots(k):
                a, b = SETS[k]
                r, n, nb = slice(0, SET_ROWS[k]), SET_ROWS[k], SET_ROWS[k] // E
                least = top[r, k, 1, CAP - 9:CAP - 8]
                step(nc.vector.tensor_scalar(isgt[r, k, :], rv[r, k, :], least, 0.0, ALU.is_gt, ALU.add,
                                             accum_out=ngt[r, k:k + 1]))
                step(nc.vector.tensor_scalar(iseq[r, k, :], rv[r, k, :], least, None, ALU.is_equal))
                step(nc.vector.tensor_tensor_scan(ceq[r, k, :], iseq[r, k, :], iseq[r, k, :], 0.0, ALU.add, ALU.bypass))
                step(nc.vector.tensor_scalar(fits[r, k, :], ceq[r, k, :], ngt[r, k:k + 1], float(CAP), ALU.add, ALU.is_le))
                step(nc.vector.tensor_tensor(fits[r, k, :], fits[r, k, :], iseq[r, k, :], ALU.mult))
                step(nc.vector.tensor_tensor(picked[r, k, :], fits[r, k, :], isgt[r, k, :], ALU.add))
                step(nc.vector.tensor_tensor_scan(cpick[r, k, :], picked[r, k, :], picked[r, k, :], 0.0, ALU.add, ALU.bypass))
                step(nc.vector.tensor_tensor(slot[r, k, :], cpick[r, k, :], picked[r, k, :], ALU.mult))
                nc.vector.tensor_tensor(lall[r, a * GB:a * GB + nb, :], slot[r, k, :].unsqueeze(1).to_broadcast([n, nb, S]),
                                        const[r, C_LM:C_LM + nb].unsqueeze(2).to_broadcast([n, nb, S]),
                                        ALU.mult).then_inc(lall_done, 1)

            def select(g):
                k = 0 if g < SETS[0][1] else 1
                dve.wait_ge(slot_ps, k + 1)
                n, m, c0 = rows(g), pics(g) * CAP, (g - SETS[k][0]) * E
                nc.vector.tensor_tensor(sel[0:n, g, 0:E * m].rearrange("p (e s) -> p e s", e=E),
                                        bank[ROUTE_BANK][0:n, c0:c0 + E].unsqueeze(2).to_broadcast([n, E, m]),
                                        const[0:n, C_PAT:C_PAT + m].unsqueeze(1).to_broadcast([n, E, m]),
                                        ALU.is_equal).then_inc(sel_done, 1)

            def take_tokens(g):
                dve.wait_ge(gather_ps, g + 1)
                n = pics(g) * CAP
                nc.vector.tensor_copy(tokT[:, :, :, g * GB * CAP:g * GB * CAP + n],
                                      bank[GATHER_BANK[g]][:, 0:2 * E * n].rearrange("p (c e s) -> p c e s", c=2, e=E)
                                      ).then_inc(gather_dve, 1)

            def take_gates(r):
                dve.wait_ge(sgt_ps, r + 1)
                for k in range(4):
                    q, g = k // 2, 2 * r + k % 2
                    n, m = rows(g), 4 * pics(g) * CAP
                    last = nc.vector.tensor_copy(sgT[0:m, q, g, 0:n], bank[GATE_BANK[r]][0:m, k * GT:k * GT + n])
                last.then_inc(sgt_done, 1)

            norm_stats(0, 0)
            norm_stats(1, 0)
            norm_apply(0, 0)
            norm_stats(2, 0)
            norm_apply(1, 0)
            norm_apply(2, 0)
            norm_stats(3, 0)
            norm_apply(3, 0)
            norm_stats(4, 0)
            spread_k(0)
            take_v(0)
            norm_apply(4, 0)
            norm_stats(5, 0)
            subtract_max(0)
            norm_apply(5, 0)
            take_v(1)
            spread_k(1)
            subtract_max(1)
            divide(0)
            take_v(2)
            subtract_max(2)
            divide(1)
            take_v(3)
            spread_k(2)
            for p in range(3, 7):
                subtract_max(p)
                divide(p - 1)
                if p >= 4:
                    norm_apply(p - 4, 1)
                take_v(p + 1)
                norm_stats(p - 3, 1)
            subtract_max(7)
            norm_apply(3, 1)
            divide(6)
            router_softmax(0)
            best_tokens(0)
            divide(7)
            number_slots(0)
            norm_stats(4, 1)
            norm_stats(5, 1)
            select(0)
            select(1)
            norm_apply(4, 1)
            norm_apply(5, 1)
            select(2)
            select(3)
            take_tokens(1)
            router_softmax(1)
            take_tokens(3)
            best_tokens(1)
            number_slots(1)
            select(4)
            select(5)
            take_gates(0)
            take_gates(1)
            take_tokens(5)
            take_gates(2)

            def take_ye(e):
                for c in range(2):
                    dve.wait_ge(f2_ps, 2 * e + c + 1)
                    bias = b2s[:, 2 * e + c:2 * e + c + 1]
                    full, m, w = (G - 1) * GB * CAP, GB * CAP, pics(G - 1) * CAP
                    nc.vector.tensor_scalar(
                        yeT[:, c, e // 4, 0:4 * full].rearrange("p (g e s) -> p g e s", g=G - 1, e=4)[:, :, e % 4, :],
                        bank[F2_BANK[c]][:, 0:full].rearrange("p (g s) -> p g s", s=m), bias, None, ALU.add)
                    nc.vector.tensor_scalar(yeT[:, c, e // 4, 4 * full + e % 4 * w:4 * full + (e % 4 + 1) * w],
                                            bank[F2_BANK[c]][:, full:SLOTS], bias, None, ALU.add).then_inc(ye_done, 1)

            def add_out(q, g):
                n = rows(g)
                dve.wait_ge(sc_ps, q * G + g + 1)
                if q == 1:
                    dve.wait_ge(ob_done, g + 1)
                nc.vector.tensor_tensor(ob[0:n, g, :], bank[SC_BANK[q][g]][0:n, 0:D],
                                        (h if q == 0 else ob)[0:n, g, :], ALU.add).then_inc(ob_done, 1)

            dve.wait_ge(in_b, 32)
            for e in range(E):
                if e == 4:
                    for g in range(G + 1):
                        if g < G:
                            dve.wait_ge(yq_ps, g + 1)
                            n = 4 * pics(g) * CAP
                            nc.vector.tensor_copy(yq[0:n, g, :], bank[YQ_BANK[0][g]][0:n, 0:D]).then_inc(yq_dve, 1)
                        if g >= 1:
                            add_out(0, g - 1)
                take_ye(e)
            for g in range(G):
                add_out(1, g)

        @block.tensor
        def _(pe):
            def mm(out_, lhsT, rhs, start=True, stop=True, **kw):
                return nc.tensor.matmul(out_, lhsT, rhs, start=start, stop=stop, **kw)

            def patches(g):
                n = rows(g)
                pe.wait_ge(in_xp[g], 16)
                if g >= 2:
                    pe.wait_ge(h_done, g - 1)
                x = xps[:, KF * GT * g:KF * GT * g + KF * n].rearrange("p (k t) -> p k t", k=KF)
                for k in range(KF):
                    if g == 0 and k % 2 == 0:
                        pe.wait_ge(in_wl[k // 2], 16)
                    last = mm(bank[PATCH_BANK[g]][0:n, 0:D], x[:, k, :], wls[:, k, :], k == 0, k == KF - 1)
                last.then_inc(patch_done, 1)

            def transpose_rows(g, norm):
                n = rows(g)
                pe.wait_ge(xn_done, norm * G + g + 1)
                if norm == 0:
                    if g == 0:
                        pe.wait_ge(in_const, 16)
                    if g == 4:
                        pe.wait_ge(q_done, 2)
                    if g == 5:
                        pe.wait_ge(k_done, 2)
                elif g == 0:
                    pe.wait_ge(k_done, UNITS)
                elif g < 4:
                    pe.wait_ge(xnt_done, G + g)
                else:
                    pe.wait_ge(h_done, G + g + 1)
                for c in range(2):
                    last = mm(bank[T_BANK[norm][g]][:, c * n:c * n + n], xn[0:n, g, c * 128:c * 128 + 128],
                              ident[0:n, 0:n], is_transpose=True)
                last.then_inc(xnt_ps, 1)

            def project(u, which, dst, done):
                n = unit_rows(u)
                t0 = 2 * GT * u
                pe.wait_ge(xnt_done, 2 * u + 2)
                if u == 1:
                    pe.wait_ge(h_done, 5 + which)
                if u == 0:
                    pe.wait_ge(in_bd, 16)
                for c in range(2):
                    last = mm(bank[dst][:, c * n:c * n + n], bds[:, which, :], xnT[:, c, t0:t0 + n])
                last.then_inc(done, 1)

            def project_q(u):
                project(u, 0, Q_BANK[u], q_ps)

            def project_k(u):
                project(u, 1, K_BANK[u], k_ps)

            def values(p):
                pe.wait_ge(xnt_done, min(G, (2 * p + 1) // GB + 1))
                if p >= 1:
                    pe.wait_ge(vb_done, p)
                for b in range(2):
                    dst = bank[V_BANK][0:GT, b * D:b * D + D].rearrange("p (f c r) -> p c f r", f=2, c=2)
                    for c in range(2):
                        last = mm(dst[:, c, :, :], xn3[:, c, 2 * p + b, :], bds[:, 2, :])
                last.then_inc(v_ps, 1)

            def scores(p):
                if p == 0:
                    pe.wait_ge(constb_ready, 1)
                else:
                    pe.wait_ge(sub_done, p)
                u = 2 * p // (2 * GB)
                pe.wait_ge(q_done, u + 1)
                pe.wait_ge(km_done, 4 * (u + 1))
                for f in range(2):
                    for b in range(2):
                        mm(bank[S_BANK[f]][64 * b:64 * b + 64, 0:8 * S], id64b[64 * f:64 * f + S, :],
                           causalb[64 * f:64 * f + S, :], True, False, skip_group_check=True)
                for c in range(2):
                    for f in range(2):
                        for b in range(2):
                            t = (2 * p + b) * S
                            last = mm(bank[S_BANK[f]][64 * b:64 * b + 64, 4 * S * c:4 * S * (c + 1)],
                                      qT[64 * f:64 * f + 64, c, 2 * p + b, :], km[64 * f:64 * f + 64, c, :, t:t + S],
                                      False, c == 1, skip_group_check=True)
                last.then_inc(s_ps, 1)

            def transpose_weights(p):
                pe.wait_ge(exp_done, p + 1)
                if p == 0:
                    pe.wait_ge(empty_heads_ready, 1)
                    pe.wait_ge(xnt_done, 3)
                else:
                    pe.wait_ge(pt_done, 2 * p)
                for t in range(TRIPLES):
                    last = mm(bank[P_BANK[t // 4]][0:GT, 128 * (t % 4):128 * (t % 4) + 128],
                              pr[:, p % 2, 3 * t:3 * t + 3, :], ident, is_transpose=True)
                last.then_inc(pt_ps, 1)

            def weigh_values(p):
                pe.wait_ge(pt_done, 2 * p + 2)
                pe.wait_ge(vb_done, p + 1)
                if p == 0:
                    pe.wait_ge(ones_ready, 1)
                    pe.wait_ge(xnt_done, 4)
                else:
                    pe.wait_ge(yt_done, p)
                for t in range(TRIPLES):
                    m = min(3, HEADS - 3 * t)
                    for b in range(2):
                        last = mm(bank[Y_BANK][64 * b:64 * b + 64, 3 * t * VC:(3 * t + m) * VC],
                                  pT[0:GT, p % 2, t, 64 * b:64 * b + 64], vb[0:GT, p % 2, b, 3 * t:3 * t + m, :])
                last.then_inc(pv_ps, 1)

            def transpose_y(p):
                pe.wait_ge(y_done, p + 1)
                for c in range(2):
                    last = mm(bank[Y_BANK][:, c * 128:c * 128 + 128], ys[:, p % 2, 8 * c:8 * c + 8, :], ident,
                              is_transpose=True)
                last.then_inc(yt_ps, 1)

            def attention_out(g):
                n = rows(g)
                if g == 0:
                    pe.wait_ge(in_wu, 16)
                    pe.wait_ge(q_done, UNITS)
                elif g < 5:
                    pe.wait_ge(h_done, G + g)
                else:
                    pe.wait_ge(lsh_done, 1)
                pe.wait_ge(yt_done, pair_needs(g))
                for c in range(2):
                    last = mm(bank[O_BANK[g]][0:n, 0:D], yT[:, c, g * GT:g * GT + n], wus[:, c, :], c == 0, c == 1)
                last.then_inc(o_ps, 1)

            def route(g):
                k = 0 if g < SETS[0][1] else 1
                pe.wait_ge(xnt_done, G + g + 1)
                if g == 0:
                    pe.wait_ge(in_rw, 16)
                if g == G - 1:
                    pe.wait_ge(xnT_pad_ready, 1)
                c0 = LOGIT_COL + (g - SETS[k][0]) * E
                for c in range(2):
                    last = mm(bank[LOGIT_BANK[k]][0:GT, c0:c0 + E], xnT[:, c, g * GT:g * GT + GT], rws[:, c, :],
                              c == 0, c == 1)
                last.then_inc(logit_ps, 1)

            def spread_router(k):
                a, b = SETS[k]
                pe.wait_ge(z_done, k + 1)
                pe.wait_ge(vb_done, PAIRS)
                if k == 1:
                    pe.wait_ge(sel_done, a)
                for g in range(a, b):
                    last = mm(bank[ROUTE_BANK][0:SET_ROWS[k], 0:S], zr[0:rows(g), g, 0:SET_ROWS[k]],
                              const[0:rows(g), C_D38:C_D38 + S], g == a, g == b - 1)
                last.then_inc(route_ps, 1)

            def slots_back(k):
                a, b = SETS[k]
                pe.wait_ge(lall_done, k + 1)
                for g in range(a, b):
                    m = pics(g)
                    last = mm(bank[ROUTE_BANK][0:rows(g), (g - a) * E:(g - a + 1) * E],
                              lall[0:SET_ROWS[k], GB * g:GB * g + m, :], e8b[0:SET_ROWS[k], :])
                last.then_inc(slot_ps, 1)

            def gather(g):
                n, m = rows(g), pics(g) * CAP
                pe.wait_ge(sel_done, g + 1)
                if g == 2:
                    pe.wait_ge(pt_done, 2 * PAIRS)
                if g == 4:
                    pe.wait_ge(sel_done, G)
                if g == 5:
                    pe.wait_ge(lsh_done, 2)
                for c in range(2):
                    last = mm(bank[GATHER_BANK[g]][:, c * E * m:c * E * m + E * m], xn[0:n, g, c * 128:c * 128 + 128],
                              sel[0:n, g, 0:E * m])
                last.then_inc(gather_ps, 1)

            chunks = [0]

            def chunk1(e, c, a, b):
                i = chunks[0]
                chunks[0] += 1
                if i >= 4:
                    pe.wait_ge(gelu_done, i - 3)
                for k in range(2):
                    last = mm(bank[F1_BANK[i % 4]][:, 0:b - a], w1s[:, e % NBUF, k, c * 128:c * 128 + 128],
                              tokT[:, k, e, a:b], k == 0, k == 1)
                last.then_inc(f1_ps, 1)

            def layer2(e):
                pe.wait_ge(in_w2[e % NBUF], 16 * (e // NBUF + 1))
                pe.wait_ge(gelu_done, f1_count(e))
                for c in range(2):
                    if e >= 1:
                        pe.wait_ge(ye_done, 2 * e - 1 + c)
                    for k in range(NH):
                        last = mm(bank[F2_BANK[c]][:, 0:SLOTS], w2s[:, e % NBUF, k, c * 128:c * 128 + 128],
                                  gT[:, e % 2, k, :], k == 0, k == NH - 1)
                    last.then_inc(f2_ps, 1)

            def transpose_gates(r):
                if r == 0:
                    pe.wait_ge(h_done, 2 * G)
                    pe.wait_ge(xnt_done, 2 * G)
                if r == 2:
                    pe.wait_ge(sgt_done, 1)
                for k in range(4):
                    q, g = k // 2, 2 * r + k % 2
                    n, m = rows(g), pics(g) * CAP
                    pe.wait_ge(selg_done, g + 1)
                    last = mm(bank[GATE_BANK[r]][0:4 * m, k * GT:k * GT + n], selg[0:n, g, 4 * q * m:4 * (q + 1) * m],
                              ident[0:n, 0:n], is_transpose=True)
                last.then_inc(sgt_ps, 1)

            def transpose_ye(q, g, c):
                m = pics(g) * CAP
                return mm(bank[YQ_BANK[q][g]][0:4 * m, c * 128:c * 128 + 128],
                          yeT[:, c, q, 4 * g * GB * CAP:4 * g * GB * CAP + 4 * m], ident, is_transpose=True)

            def scatter(q, g):
                n, m = rows(g), 4 * pics(g) * CAP
                mm(bank[SC_BANK[q][g]][0:n, 0:D], sgT[0:m, q, g, 0:n], yq[0:m, g, :]).then_inc(sc_ps, 1)

            patches(0)
            patches(1)
            patches(2)
            transpose_rows(0, 0)
            patches(3)
            transpose_rows(1, 0)
            transpose_rows(2, 0)
            patches(4)
            project_q(0)
            project_k(0)
            transpose_rows(3, 0)
            values(0)
            patches(5)
            scores(0)
            values(1)
            project_q(1)
            project_k(1)
            transpose_weights(0)
            scores(1)
            weigh_values(0)
            values(2)
            transpose_rows(4, 0)
            transpose_y(0)
            transpose_weights(1)
            transpose_rows(5, 0)
            scores(2)
            weigh_values(1)
            values(3)
            project_q(2)
            project_k(2)
            transpose_y(1)
            transpose_weights(2)
            for p in range(3, 7):
                scores(p)
                weigh_values(p - 1)
                if p >= 5:
                    route(p - 5)
                values(p + 1)
                transpose_y(p - 1)
                transpose_weights(p)
                if p >= 4:
                    transpose_rows(p - 4, 1)
                attention_out(p - 3)
            scores(7)
            weigh_values(6)
            route(2)
            transpose_rows(3, 1)
            transpose_weights(7)
            transpose_y(6)
            route(3)
            weigh_values(7)
            spread_router(0)
            transpose_y(7)
            attention_out(4)
            attention_out(5)
            slots_back(0)
            gather(0)
            gather(1)
            transpose_rows(4, 1)
            transpose_rows(5, 1)
            gather(2)
            route(4)
            route(5)
            gather(3)
            spread_router(1)

            pe.wait_ge(in_w1[0], 16)
            pe.wait_ge(gather_act, 2)
            pe.wait_ge(gather_dve, 2)
            for c in range(NH):
                chunk1(0, c, 0, SLOTS_A)
            slots_back(1)
            transpose_gates(0)
            transpose_gates(1)
            gather(4)
            gather(5)
            pe.wait_ge(gather_act, 3)
            pe.wait_ge(gather_dve, 3)
            for c in range(NH):
                chunk1(0, c, SLOTS_A, SLOTS)
            transpose_gates(2)
            for e in range(E):
                if e + 1 < E:
                    pe.wait_ge(in_w1[(e + 1) % NBUF], 16 * ((e + 1) // NBUF + 1))
                    for c in range(NH):
                        chunk1(e + 1, c, 0, SLOTS)
                        if e == 4 and c == 0:
                            pe.wait_ge(sgt_done, 3)
                            pe.wait_ge(ye_done, 8)
                        if e == 4 and 1 <= c <= G:
                            pe.wait_ge(yq_dve, c)
                            if c >= 2:
                                pe.wait_ge(ob_done, c - 1)
                            scatter(0, c - 1)
                        if e == 4 and c < G:
                            if c >= 1:
                                pe.wait_ge(yq_dve, c)
                            transpose_ye(0, c, 0)
                            transpose_ye(0, c, 1).then_inc(yq_ps, 1)
                layer2(e)
            pe.wait_ge(gelu_done, f1_count(E - 1))
            pe.wait_ge(ob_done, G)
            pe.wait_ge(ye_done, 2 * E - 1)
            for g in range(G):
                transpose_ye(1, g, 0)
            pe.wait_ge(ye_done, 2 * E)
            for g in range(G):
                transpose_ye(1, g, 1).then_inc(yq_ps, 1)
            for g in range(G):
                pe.wait_ge(yq_act, max(g + 1, 3 if g >= 2 else 0))
                if g >= 4:
                    pe.wait_ge(ob_done, G + g - 3)
                scatter(1, g)


def shape_constants():
    import numpy as np
    c = np.zeros((128, C_END), np.float32)
    p = np.arange(128)
    c[:, C_ID:C_ID + 128] = np.eye(128)
    for m in range(4):
        c[:, C_KM + m] = 0.25 * ((p % 64) // HC == m)
    for i in range(HEADS):
        c[:, C_M3 + i] = p // S == i % 3
    for b in range(GB):
        for s in range(CAP):
            c[:, C_PAT + b * CAP + s] = np.where(p // S == b, s + 1, -1)
        c[:, C_ZM + b] = p // S == b
    for s in range(S):
        c[:, C_D38 + s] = p % S == s
    for b in range(SETS[0][1] * GB):
        c[:, C_LM + b] = p // E == b
    for e in range(E):
        c[:, C_E8 + e] = p % E == e
    for r in (0, 64):
        for i in range(S):
            c[r + i, C_I64 + i] = 1
    for r in (0, 64):
        for i in range(S):
            for hd in range(8):
                c[r + i, C_CM + hd * S + i + 1:C_CM + hd * S + S] = MASKED
    return c


def kernel(x, cls_tok, L0_tok_W_lin, L0_tok_b_lin, L0_tok_class_token, L0_tok_position_embeddings, L0_attn_Wq,
           L0_attn_Wk, L0_attn_Wv, L0_attn_Wu, L0_attn_bu, L0_ffn_router_w, L0_ffn_w1, L0_ffn_b1, L0_ffn_w2,
           L0_ffn_b2):
    import numpy as np
    import concourse.bacc as bacc
    from concourse.bass_utils import run_bass_kernel_spmd

    a = lambda v: np.ascontiguousarray(np.asarray(v))
    side = IMG // PATCH
    xf = a(x).reshape(B, C_IN, side, PATCH, side, PATCH).transpose(1, 3, 5, 0, 2, 4).reshape(F, B, NPATCH)
    xt = np.zeros((F, B, S), np.float32)
    xt[:, :, 2:] = xf
    xt = xt.reshape(KF, 128, TOK)
    xp = np.concatenate([xt[:, :, g * GT:g * GT + rows(g)].transpose(1, 0, 2).reshape(128, -1) for g in range(G)], axis=1)
    wl = a(L0_tok_W_lin).T.reshape(KF, 128, D).transpose(1, 0, 2)
    one_a = np.concatenate([a(cls_tok).reshape(1, D), a(L0_tok_position_embeddings).reshape(S - 1, D)])
    one_b = np.concatenate([np.zeros((1, D), np.float32), a(L0_tok_class_token).reshape(1, D),
                            np.repeat(a(L0_tok_b_lin).reshape(1, D), NPATCH, axis=0)])
    rows_a, rows_b = (np.resize(v, (128, D)) for v in (one_a, one_b))
    bd = np.zeros((128, 3, 128), np.float32)
    for w, m in enumerate((L0_attn_Wq, L0_attn_Wk, L0_attn_Wv)):
        for i in range(128 // HC):
            bd[i * HC:(i + 1) * HC, w, i * HC:(i + 1) * HC] = a(m).T
    wu = a(L0_attn_Wu).T.reshape(2, 128, D).transpose(1, 0, 2)
    bu = np.repeat(a(L0_attn_bu).reshape(1, D), 128, axis=0)
    rw = a(L0_ffn_router_w).T.reshape(2, 128, E).transpose(1, 0, 2)
    w1 = a(L0_ffn_w1).reshape(E, 2, 128, HID).transpose(0, 2, 1, 3)
    b1 = a(L0_ffn_b1).reshape(E * NH, 128).T
    w2 = a(L0_ffn_w2).reshape(E, NH, 128, D).transpose(0, 2, 1, 3)
    b2 = a(L0_ffn_b2).reshape(E * 2, 128).T
    arrays = dict(xp=xp, wl=wl, rows_a=rows_a, rows_b=rows_b, bd=bd, wu=wu, bu=bu, rw=rw, w1=w1, b1=b1, w2=w2, b2=b2,
                  consts=shape_constants())
    arrays = {f"{n}_dram": np.ascontiguousarray(v) for n, v in arrays.items()}

    nc = bacc.Bacc("TRN2", target_bir_lowering=False, num_devices=1)
    args = [nc.dram_tensor(n, v.shape, mybir.dt.float32, kind="ExternalInput").ap() for n, v in arrays.items()]
    out = nc.dram_tensor("out_dram", (TOK, D), mybir.dt.float32, kind="ExternalOutput").ap()
    tower(nc, *args, out)
    r = run_bass_kernel_spmd(nc, [arrays], core_ids=[0])
    return r.results[0]["out_dram"].reshape(B, S, D)
```

```python
from contextlib import ExitStack

import concourse.bass as bass
from concourse import mybir

B, C_IN, IMG, PATCH = 16, 3, 96, 16
D, HEADS, HC = 256, 16, 16
NPATCH = (IMG // PATCH) ** 2
S = NPATCH + 2
TOK = B * S
F = C_IN * PATCH * PATCH
KF = F // 128
E, HID = 8, 1024
NH = HID // 128
CAP = max(1, int(S * 2.0 / E) + 1)
SLOTS = B * CAP

GB = 3
GT = GB * S
G = -(-B // GB)
GTP = G * GT
PAIRS = B // 2
UNITS = G // 2
QW = 64
POS = 18
TRIPLES = POS // 3
VC = HC + 1
NBUF = 4
MASKED = -1e30
WARM, WARM_UP = 256, 3
SETS = ((0, G // 2), (G // 2, G))
SET_ROWS = [(min(b * GB, B) - a * GB) * E for a, b in SETS]
SLOTS_A = SETS[0][1] * GB * CAP

C_ID, C_KM, C_M3, C_PAT, C_ZM, C_D38, C_LM, C_E8, C_I64 = 0, 128, 132, 148, 178, 181, 219, 231, 239
C_CM = C_I64 + 64
C_END = C_CM + 8 * S


def rows(g):
    return min(GT, TOK - g * GT)


def pics(g):
    return min(GB, B - g * GB)


def unit_rows(u):
    return min(2 * GT, TOK - 2 * GT * u)


def pair_needs(g):
    return min(PAIRS, (GB * (g + 1) + 1) // 2)


def tower(nc, xp, wl, rows_a, rows_b, bd, wu, bu, rw, w1, b1, w2, b2, consts, out):
    fp32, bf16 = mybir.dt.float32, mybir.dt.bfloat16
    ALU, ACT, AX = mybir.AluOpType, mybir.ActivationFunctionType, mybir.AxisListType

    with ExitStack() as ctx:
        def sb(name, shape, dt=fp32):
            return ctx.enter_context(nc.sbuf_tensor(name, shape, dt))

        def sem(name):
            return ctx.enter_context(nc.semaphore(name))

        const = sb("const", [128, C_END])
        ident = const[:, C_ID:C_ID + 128]
        constb = sb("constb", [128, C_END - C_E8], bf16)
        e8b = constb[:, 0:8]
        id64b = constb[:, C_I64 - C_E8:C_I64 - C_E8 + 64]
        causalb = constb[:, C_CM - C_E8:C_CM - C_E8 + 8 * S]
        xps = sb("xps", [128, KF * TOK])
        wls = sb("wls", [128, KF, D])
        add_a = sb("add_a", [128, D])
        add_b = sb("add_b", [128, D])
        bds = sb("bds", [128, 3, 128])
        wus = sb("wus", [128, 2, D])
        bus = sb("bus", [128, D])
        rws = sb("rws", [128, 2, E])
        b1s = sb("b1s", [128, E * NH])
        b2s = sb("b2s", [128, E * 2])
        w1s = sb("w1s", [128, NBUF, 2, HID])
        w2s = sb("w2s", [128, NBUF, NH, D])
        h = sb("h", [128, G, D])
        hb = sb("hb", [128, G, D])
        xn = sb("xn", [128, G, D])
        stat = sb("stat", [128, G, 6])
        mv = sb("mv", [128, G, 2])
        ve = sb("ve", [128, G])
        lnv = sb("lnv", [128, G])
        r0 = sb("r0", [128, G])
        nt = sb("nt", [128, G, 2])
        rstd = sb("rstd", [128, G])
        xnT = sb("xnT", [128, 2, GTP])
        qT = sb("qT", [128, 2, B, QW])
        kf = sb("kf", [128, 2, 2, 2 * GT])
        km = sb("km", [128, 2, 4, TOK])
        vb = sb("vb", [128, 2, 2, HEADS, VC])
        mx = sb("mx", [128, 2, HEADS])
        pr = sb("pr", [128, 2, POS, S])
        pT = sb("pT", [128, 2, TRIPLES, 128])
        rs = sb("rs", [128, 2, HEADS])
        ys = sb("ys", [128, 2, HEADS, HC])
        yT = sb("yT", [128, 2, TOK])
        rmax = sb("rmax", [128, G])
        lsh = sb("lsh", [128, G, E])
        lex = sb("lex", [128, G, E])
        rsum = sb("rsum", [128, G])
        rrec = sb("rrec", [128, G])
        sc = sb("sc", [128, G, E])
        zr = sb("zr", [128, G, SET_ROWS[0]])
        rv2 = sb("rv2", [128, 2, S])
        top = sb("top", [128, 2, 2, 8])
        isgt = sb("isgt", [128, 2, S])
        ngt = sb("ngt", [128, 2])
        iseq = sb("iseq", [128, 2, S])
        ceq = sb("ceq", [128, 2, S])
        fits = sb("fits", [128, 2, S])
        picked = sb("picked", [128, 2, S])
        cpick = sb("cpick", [128, 2, S])
        slot = sb("slot", [128, 2, S])
        lall = sb("lall", [128, G * GB, S], bf16)
        shared = sb("shared", [128, 2 * B * GT])
        xn3 = shared[:, :].rearrange("p (c b r) -> p c b r", c=2, b=B)
        sel = shared[:, 0:G * E * GB * CAP].rearrange("p (g s) -> p g s", g=G)
        selg = shared[:, G * E * GB * CAP:2 * G * E * GB * CAP].rearrange("p (g s) -> p g s", g=G)
        tokT = sb("tokT", [128, 2, E, SLOTS])
        gT = km[:].rearrange("p c m t -> p (c m t)")[:, 0:2 * NH * SLOTS].rearrange("p (b k s) -> p b k s", b=2, k=NH)
        yeT = xps[:, 0:2 * E * SLOTS].rearrange("p (c q s) -> p c q s", c=2, q=2)
        sgT = pT[:].rearrange("p b t n -> p (b t n)")[:, 0:2 * G * GT].rearrange("p (q g t) -> p q g t", q=2, g=G)
        yq = wls
        ob = hb

        bank = [ctx.enter_context(nc.psum_tensor(f"bank{i}", [128, 512], fp32)) for i in range(8)]
        S_BANK, V_BANK, P_BANK, Y_BANK = (0, 1), 2, (3, 4), 5
        WARM_BANK = 0
        PATCH_BANK = (6, 7, 6, 7, 6, 7)
        T_BANK = ((2, 3, 4, 5, 6, 7), (7, 7, 7, 1, 6, 7))
        Q_BANK, K_BANK = (0, 6, 6), (1, 7, 7)
        O_BANK = (6, 6, 6, 6, 6, 7)
        LOGIT_BANK, LOGIT_COL = (7, 5), 256
        ROUTE_BANK = 2
        GATHER_BANK = (0, 1, 3, 6, 2, 5)
        F1_BANK, F2_BANK = (0, 1, 3, 4), (2, 5)
        GATE_BANK = (7, 6, 7)
        YQ_BANK = ((5, 6) * (G // 2), (0, 1, 3, 4, 6, 7))
        SC_BANK = ((2, 7) * (G // 2), (2, 5, 0, 1, 2, 5))

        in_const, in_rows, in_bd, in_wu, in_bu, in_rw, in_b = (
            sem(n) for n in ("in_const", "in_rows", "in_bd", "in_wu", "in_bu", "in_rw", "in_b"))
        in_wl = [sem(f"in_wl{i}") for i in range(3)]
        in_xp = [sem(f"in_xp{g}") for g in range(G)]
        in_w1 = [sem(f"in_w1_{i}") for i in range(NBUF)]
        in_w2 = [sem(f"in_w2_{i}") for i in range(NBUF)]
        (constb_ready, rows_ready, qpad_ready, empty_heads_ready, xnT_pad_ready, ones_ready, zr_ready, hb_done,
         selg_done) = (
            sem(n) for n in ("constb_ready", "rows_ready", "qpad_ready", "empty_heads_ready", "xnT_pad_ready",
                             "ones_ready", "zr_ready", "hb_done", "selg_done"))
        (patch_done, xnt_ps, q_ps, k_ps, v_ps, s_ps, pt_ps, pv_ps, yt_ps, o_ps, logit_ps, route_ps, slot_ps,
         gather_ps, sgt_ps, f1_ps, f2_ps, yq_ps, sc_ps) = (
            sem(n) for n in ("patch_done", "xnt_ps", "q_ps", "k_ps", "v_ps", "s_ps", "pt_ps", "pv_ps", "yt_ps",
                             "o_ps", "logit_ps", "route_ps", "slot_ps", "gather_ps", "sgt_ps", "f1_ps", "f2_ps",
                             "yq_ps", "sc_ps"))
        warm_ready = sem("warm_ready")
        (h_done, stats_done, mv_done, ve_done, nt_done, rstd_done, xn_done, km_done, vb_done, mx_done, sub_done,
         rs_done, y_done, soft_done, lsh_done, sc_done, z_done, topk_done, lall_done, sel_done, sgt_done, ye_done,
         ob_done, gather_dve, yq_dve) = (
            sem(n) for n in ("h_done", "stats_done", "mv_done", "ve_done", "nt_done", "rstd_done", "xn_done",
                             "km_done", "vb_done", "mx_done", "sub_done", "rs_done", "y_done", "soft_done",
                             "lsh_done", "sc_done", "z_done", "topk_done", "lall_done", "sel_done", "sgt_done",
                             "ye_done", "ob_done", "gather_dve", "yq_dve"))
        (ln_done, r0_done, xnt_done, q_done, k_done, exp_done, pt_done, yt_done, lex_done, gather_act,
         gelu_done, yq_act) = (
            sem(n) for n in ("ln_done", "r0_done", "xnt_done", "q_done", "k_done", "exp_done", "pt_done", "yt_done",
                             "lex_done", "gather_act", "gelu_done", "yq_act"))
        stored = sem("stored")

        def f1_count(e):
            return 3 * NH - 1 if e == 0 else NH * (e + 2)

        block = ctx.enter_context(nc.Block())

        @block.sync
        def _(sp):
            for i in range(3):
                sp.dma_start(wls[:, 2 * i:2 * i + 2, :], wl[:, 2 * i:2 * i + 2, :]).then_inc(in_wl[i], 16)
            for g in range(1, G):
                a = KF * GT * g
                sp.dma_start(xps[:, a:a + KF * rows(g)], xp[:, a:a + KF * rows(g)]).then_inc(in_xp[g], 16)
            sp.dma_start(wus[:], wu).then_inc(in_wu, 16)
            sp.dma_start(rws[:], rw).then_inc(in_rw, 16)
            sp.dma_start(b1s[:], b1).then_inc(in_b, 16)
            sp.dma_start(b2s[:], b2).then_inc(in_b, 16)
            for e in range(E):
                if e >= NBUF:
                    sp.wait_ge(f1_ps, f1_count(e - NBUF))
                sp.dma_start(w1s[:, e % NBUF, :, :], w1[e, :, :, :]).then_inc(in_w1[e % NBUF], 16)
                if e >= NBUF:
                    sp.wait_ge(f2_ps, 2 * (e - NBUF + 1))
                sp.dma_start(w2s[:, e % NBUF, :, :], w2[e, :, :, :]).then_inc(in_w2[e % NBUF], 16)
            for g in range(G):
                sp.wait_ge(ob_done, G + g + 1)
                sp.dma_start(out[g * GT:g * GT + rows(g), :], ob[0:rows(g), g, :]).then_inc(stored, 16)
            sp.wait_ge(stored, 16 * G)

        @block.gpsimd
        def _(pool):
            nc.gpsimd.memset(qT[:, :, :, S:QW], 0.0).then_inc(qpad_ready, 1)
            nc.gpsimd.memset(pr[:, :, HEADS:POS, :], 0.0).then_inc(empty_heads_ready, 1)
            nc.gpsimd.memset(xnT[:, :, TOK:GTP], 0.0).then_inc(xnT_pad_ready, 1)
            pool.wait_ge(in_rows, 32)
            nc.gpsimd.tensor_tensor(add_a[:], add_a[:], add_b[:], ALU.add).then_inc(rows_ready, 1)
            pool.wait_ge(in_const, 16)
            nc.gpsimd.tensor_copy(constb[:], const[:, C_E8:C_END]).then_inc(constb_ready, 1)
            nc.gpsimd.tensor_copy(
                vb[:, :, :, :, HC], const[:, C_M3:C_M3 + HEADS].unsqueeze(1).unsqueeze(1).to_broadcast([128, 2, 2, HEADS])
            ).then_inc(ones_ready, 1)
            nc.gpsimd.memset(zr[:], 0.0).then_inc(zr_ready, 1)
            pool.wait_ge(in_bu, 16)
            for g in range(G):
                pool.wait_ge(h_done, g + 1)
                nc.gpsimd.tensor_tensor(hb[0:rows(g), g, :], h[0:rows(g), g, :], bus[0:rows(g), :],
                                        ALU.add).then_inc(hb_done, 1)
            for g in range(G):
                pool.wait_ge(sel_done, g + 1)
                pool.wait_ge(sc_done, 1 if g < SETS[0][1] else 2)
                n = pics(g) * CAP
                nc.gpsimd.tensor_tensor(
                    selg[0:rows(g), g, 0:E * n].rearrange("p (e s) -> p e s", e=E),
                    sel[0:rows(g), g, 0:E * n].rearrange("p (e s) -> p e s", e=E),
                    sc[0:rows(g), g, :].unsqueeze(2).to_broadcast([rows(g), E, n]), ALU.mult).then_inc(selg_done, 1)

        @block.scalar
        def _(act):
            act.dma_start(xps[:, 0:KF * rows(0)], xp[:, 0:KF * rows(0)]).then_inc(in_xp[0], 16)
            act.dma_start(add_a[:], rows_a).then_inc(in_rows, 16)
            act.dma_start(add_b[:], rows_b).then_inc(in_rows, 16)
            act.dma_start(const[:], consts).then_inc(in_const, 16)
            act.dma_start(bds[:], bd).then_inc(in_bd, 16)
            act.dma_start(bus[:], bu).then_inc(in_bu, 16)
            nc.scalar.preload_act_table_set("natural_log_exp_and_others")

            def first_rstd(g, norm):
                n = rows(g)
                act.wait_ge(ve_done, norm * G + g + 1)
                nc.scalar.activation(lnv[0:n, g:g + 1], ve[0:n, g:g + 1], ACT.Ln).then_inc(ln_done, 1)
                act.wait_ge(ln_done, norm * G + g + 1)
                nc.scalar.activation(r0[0:n, g:g + 1], lnv[0:n, g:g + 1], ACT.Exp, scale=-0.5).then_inc(r0_done, 1)

            def take_xnT(g, norm):
                n, m = rows(g), pics(g)
                act.wait_ge(xnt_ps, norm * G + g + 1)
                src = bank[T_BANK[norm][g]][:, 0:2 * n].rearrange("p (c t) -> p c t", c=2)
                if norm == 0:
                    for c in range(2):
                        nc.scalar.activation(
                            xn3[:, c, g * GB:g * GB + m, :].rearrange("p b (r t) -> p b r t", r=3),
                            src[:, c, :].rearrange("p (b t) -> p b t", t=S).unsqueeze(2).to_broadcast([128, m, 3, S]),
                            ACT.Copy)
                nc.scalar.activation(xnT[:, :, g * GT:g * GT + n], src, ACT.Copy).then_inc(xnt_done, 1)

            def take_q(u):
                n = unit_rows(u)
                b0 = 2 * GB * u
                if u == 0:
                    act.wait_ge(qpad_ready, 1)
                act.wait_ge(q_ps, u + 1)
                nc.scalar.activation(qT[:, :, b0:b0 + n // S, 0:S],
                                     bank[Q_BANK[u]][:, 0:2 * n].rearrange("p (c b t) -> p c b t", c=2, t=S),
                                     ACT.Copy, scale=0.25).then_inc(q_done, 1)

            def take_k(u):
                n = unit_rows(u)
                act.wait_ge(k_ps, u + 1)
                if u >= 2:
                    act.wait_ge(km_done, 4 * (u - 1))
                nc.scalar.activation(kf[:, u % 2, :, 0:n],
                                     bank[K_BANK[u]][:, 0:2 * n].rearrange("p (c t) -> p c t", c=2),
                                     ACT.Copy).then_inc(k_done, 1)

            def take_pT(p):
                act.wait_ge(pt_ps, p + 1)
                if p >= 2:
                    act.wait_ge(pv_ps, p - 1)
                nc.scalar.activation(pT[0:GT, p % 2, 0:4, :],
                                     bank[P_BANK[0]][0:GT, :].rearrange("p (t n) -> p t n", t=4),
                                     ACT.Copy).then_inc(pt_done, 1)
                nc.scalar.activation(pT[0:GT, p % 2, 4:6, :],
                                     bank[P_BANK[1]][0:GT, 0:256].rearrange("p (t n) -> p t n", t=2),
                                     ACT.Copy).then_inc(pt_done, 1)

            def take_yT(p):
                act.wait_ge(yt_ps, p + 1)
                nc.scalar.activation(
                    yT[:, :, 2 * p * S:2 * (p + 1) * S].rearrange("p c (b t) -> p c b t", b=2),
                    bank[Y_BANK][:, 0:256].rearrange("p (c b t) -> p c b t", c=2, b=2)[:, :, :, 0:S],
                    ACT.Copy).then_inc(yt_done, 1)

            def weights(p):
                act.wait_ge(sub_done, p + 1)
                nc.scalar.activation(pr[:, p % 2, 0:HEADS, :], pr[:, p % 2, 0:HEADS, :], ACT.Exp).then_inc(exp_done, 1)

            def router_exp(k):
                a, b = SETS[k]
                act.wait_ge(lsh_done, k + 1)
                nc.scalar.activation(lex[0:GT, a:b, :], lsh[0:GT, a:b, :], ACT.Exp).then_inc(lex_done, 1)

            def take_tokens(g):
                act.wait_ge(gather_ps, g + 1)
                n = pics(g) * CAP
                nc.scalar.activation(tokT[:, :, :, g * GB * CAP:g * GB * CAP + n],
                                     bank[GATHER_BANK[g]][:, 0:2 * E * n].rearrange("p (c e s) -> p c e s", c=2, e=E),
                                     ACT.Copy).then_inc(gather_act, 1)

            first_rstd(0, 0)
            first_rstd(1, 0)
            first_rstd(2, 0)
            take_xnT(0, 0)
            take_xnT(1, 0)
            first_rstd(3, 0)
            take_q(0)
            take_k(0)
            first_rstd(4, 0)
            take_xnT(2, 0)
            take_xnT(3, 0)
            first_rstd(5, 0)
            weights(0)
            take_q(1)
            take_k(1)
            take_pT(0)
            weights(1)
            take_xnT(4, 0)
            take_yT(0)
            take_pT(1)
            take_xnT(5, 0)
            weights(2)
            take_q(2)
            take_yT(1)
            take_pT(2)
            for p in range(3, 7):
                if p >= 4:
                    first_rstd(p - 4, 1)
                weights(p)
                if p == 3:
                    take_k(2)
                take_yT(p - 1)
                if p >= 4:
                    take_xnT(p - 4, 1)
                take_pT(p)
            weights(7)
            router_exp(0)
            take_pT(7)
            take_yT(6)
            first_rstd(3, 1)
            take_yT(7)
            take_xnT(3, 1)
            first_rstd(4, 1)
            first_rstd(5, 1)
            take_tokens(0)
            take_xnT(4, 1)
            take_xnT(5, 1)
            take_tokens(2)
            router_exp(1)

            act.wait_ge(in_b, 32)

            def gelu(e, c, a, b):
                i = chunks[0]
                chunks[0] += 1
                act.wait_ge(f1_ps, i + 1)
                nc.scalar.activation(gT[:, e % 2, c, a:b], bank[F1_BANK[i % 4]][:, 0:b - a], ACT.Gelu,
                                     bias=b1s[:, e * NH + c:e * NH + c + 1]).then_inc(gelu_done, 1)

            chunks = [0]
            for c in range(NH):
                gelu(0, c, 0, SLOTS_A)
            take_tokens(4)
            for c in range(NH):
                gelu(0, c, SLOTS_A, SLOTS)
                gelu(1, c, 0, SLOTS)
            with act.Fori(1, E // 2) as pair:
                for e in range(2):
                    act.wait_ge(f2_ps, 4 * pair + (2 * e - 2))
                    for c in range(NH):
                        act.wait_ge(f1_ps, 2 * NH * pair + (NH * (e + 1) + c + 1))
                        nc.scalar.activation(gT[:, e, c, :], bank[F1_BANK[c % 4]][:, 0:SLOTS], ACT.Gelu,
                                             bias=b1s[:, bass.ds(2 * NH * pair + (NH * e + c), 1)]).then_inc(gelu_done, 1)
            for g in range(G):
                act.wait_ge(yq_ps, G + g + 1)
                act.wait_ge(sc_ps, g + 1)
                n = 4 * pics(g) * CAP
                nc.scalar.activation(yq[0:n, g, :], bank[YQ_BANK[1][g]][0:n, 0:D], ACT.Copy).then_inc(yq_act, 1)

        @block.vector
        def _(dve):
            def add_rows(g, norm):
                n = rows(g)
                if norm == 0:
                    dve.wait_ge(patch_done, g + 1)
                    dve.wait_ge(rows_ready, 1)
                    nc.vector.tensor_tensor(h[0:n, g, :], bank[PATCH_BANK[g]][0:n, 0:D], add_a[0:n, :],
                                            ALU.add).then_inc(h_done, 1)
                else:
                    dve.wait_ge(o_ps, g + 1)
                    dve.wait_ge(hb_done, g + 1)
                    nc.vector.tensor_tensor(h[0:n, g, :], bank[O_BANK[g]][0:n, 0:D], hb[0:n, g, :],
                                            ALU.add).then_inc(h_done, 1)

            def row_stats(g, norm):
                n = rows(g)
                dve.wait_ge(h_done, norm * G + g + 1)
                nc.vector.bn_stats(stat[0:n, g, :], h[0:n, g, :]).then_inc(stats_done, 1)

            def mean_var(g, norm):
                n = rows(g)
                dve.wait_ge(stats_done, norm * G + g + 1)
                nc.vector.bn_aggr(mv[0:n, g, :], stat[0:n, g, :]).then_inc(mv_done, 1)

            def var_eps(g, norm):
                n = rows(g)
                dve.wait_ge(mv_done, norm * G + g + 1)
                nc.vector.tensor_scalar(ve[0:n, g:g + 1], mv[0:n, g, 1:2], 1e-5, None, ALU.add).then_inc(ve_done, 1)

            def newton_square(g, norm):
                n = rows(g)
                dve.wait_ge(r0_done, norm * G + g + 1)
                nc.vector.scalar_tensor_tensor(nt[0:n, g, 0:1], r0[0:n, g:g + 1], ve[0:n, g:g + 1], r0[0:n, g:g + 1],
                                               ALU.mult, ALU.mult).then_inc(nt_done, 1)

            def newton_factor(g, norm):
                n = rows(g)
                dve.wait_ge(nt_done, 2 * (norm * G + g) + 1)
                nc.vector.tensor_scalar(nt[0:n, g, 1:2], nt[0:n, g, 0:1], -0.5, 1.5, ALU.mult, ALU.add).then_inc(nt_done, 1)

            def newton_apply(g, norm):
                n = rows(g)
                dve.wait_ge(nt_done, 2 * (norm * G + g) + 2)
                nc.vector.tensor_tensor(rstd[0:n, g:g + 1], r0[0:n, g:g + 1], nt[0:n, g, 1:2], ALU.mult).then_inc(rstd_done, 1)

            def normalise(g, norm):
                n = rows(g)
                dve.wait_ge(rstd_done, norm * G + g + 1)
                if norm == 1:
                    dve.wait_ge(xnt_ps, G)
                dst, src = xn[0:n, g, :], h[0:n, g, :]
                if norm == 0:
                    dst = dst.rearrange("p (c f r) -> p c f r", c=2, f=2)
                    src = src.rearrange("p (f c r) -> p c f r", c=2, f=2)
                nc.vector.tensor_scalar(dst, src, mv[0:n, g, 0:1], rstd[0:n, g:g + 1],
                                        ALU.subtract, ALU.mult).then_inc(xn_done, 1)

            def norm_stats(g, norm):
                add_rows(g, norm)
                row_stats(g, norm)
                mean_var(g, norm)
                var_eps(g, norm)

            def norm_apply(g, norm):
                newton_square(g, norm)
                newton_factor(g, norm)
                newton_apply(g, norm)
                normalise(g, norm)

            def spread_k(u):
                n = unit_rows(u)
                t0 = 2 * GT * u
                dve.wait_ge(k_done, u + 1)
                for m in range(4):
                    nc.vector.tensor_scalar(km[:, :, m, t0:t0 + n], kf[:, u % 2, :, 0:n],
                                            const[:, C_KM + m:C_KM + m + 1], None, ALU.mult).then_inc(km_done, 1)

            def subtract_max(p):
                dve.wait_ge(s_ps, p + 1)
                for f in range(2):
                    nc.vector.tensor_reduce(mx[:, p % 2, 8 * f:8 * f + 8],
                                            bank[S_BANK[f]][:, 0:8 * S].rearrange("p (h t) -> p h t", h=8), AX.X,
                                            ALU.max).then_inc(mx_done, 1)
                if p >= 2:
                    dve.wait_ge(pt_ps, p - 1)
                for f in range(2):
                    dve.wait_ge(mx_done, 2 * p + f + 1)
                    last = nc.vector.tensor_tensor(
                        pr[:, p % 2, 8 * f:8 * f + 8, :],
                        bank[S_BANK[f]][:, 0:8 * S].rearrange("p (h t) -> p h t", h=8),
                        mx[:, p % 2, 8 * f:8 * f + 8].unsqueeze(2).to_broadcast([128, 8, S]), ALU.subtract)
                last.then_inc(sub_done, 1)

            def take_v(p):
                dve.wait_ge(v_ps, p + 1)
                if p >= 2:
                    dve.wait_ge(pv_ps, p - 1)
                nc.vector.tensor_tensor(
                    vb[0:GT, p % 2, :, :, 0:HC], bank[V_BANK][0:GT, :].rearrange("p (b h c) -> p b h c", b=2, h=HEADS),
                    const[0:GT, C_M3:C_M3 + HEADS].unsqueeze(1).unsqueeze(3).to_broadcast([GT, 2, HEADS, HC]),
                    ALU.mult).then_inc(vb_done, 1)

            def weight_sums(p):
                dve.wait_ge(pv_ps, p + 1)
                nc.vector.reciprocal(rs[:, p % 2, :], pair_y()[:, :, HC]).then_inc(rs_done, 1)

            def divide_y(p):
                dve.wait_ge(rs_done, p + 1)
                if p >= 2:
                    dve.wait_ge(yt_ps, p - 1)
                nc.vector.tensor_tensor(ys[:, p % 2, :, :], pair_y()[:, :, 0:HC],
                                        rs[:, p % 2, :].unsqueeze(2).to_broadcast([128, HEADS, HC]),
                                        ALU.mult).then_inc(y_done, 1)

            def pair_y():
                return bank[Y_BANK][:, 0:HEADS * VC].rearrange("p (h c) -> p h c", h=HEADS)

            def divide(p):
                weight_sums(p)
                divide_y(p)

            def set_logits(k):
                w = SETS[k][1] - SETS[k][0]
                return bank[LOGIT_BANK[k]][0:GT, LOGIT_COL:LOGIT_COL + w * E].rearrange("p (g e) -> p g e", e=E)

            def router_max(k):
                a, b = SETS[k]
                dve.wait_ge(logit_ps, b)
                nc.vector.tensor_reduce(rmax[0:GT, a:b], set_logits(k), AX.X, ALU.max).then_inc(soft_done, 1)

            def router_shift(k):
                a, b = SETS[k]
                dve.wait_ge(soft_done, 3 * k + 1)
                nc.vector.tensor_tensor(lsh[0:GT, a:b, :], set_logits(k),
                                        rmax[0:GT, a:b].unsqueeze(2).to_broadcast([GT, b - a, E]),
                                        ALU.subtract).then_inc(lsh_done, 1)

            def router_sum(k):
                a, b = SETS[k]
                dve.wait_ge(lex_done, k + 1)
                nc.vector.tensor_reduce(rsum[0:GT, a:b], lex[0:GT, a:b, :], AX.X, ALU.add).then_inc(soft_done, 1)

            def router_reciprocal(k):
                a, b = SETS[k]
                dve.wait_ge(soft_done, 3 * k + 2)
                nc.vector.reciprocal(rrec[0:GT, a:b], rsum[0:GT, a:b]).then_inc(soft_done, 1)

            def router_divide(k):
                a, b = SETS[k]
                dve.wait_ge(soft_done, 3 * k + 3)
                nc.vector.tensor_tensor(sc[0:GT, a:b, :], lex[0:GT, a:b, :],
                                        rrec[0:GT, a:b].unsqueeze(2).to_broadcast([GT, b - a, E]),
                                        ALU.mult).then_inc(sc_done, 1)

            def router_columns(k):
                a, b = SETS[k]
                dve.wait_ge(soft_done, 3 * k + 3)
                if k == 0:
                    dve.wait_ge(zr_ready, 1)
                for g in range(a, b):
                    n, m, c0 = rows(g), pics(g), (g - a) * GB * E
                    last = nc.vector.scalar_tensor_tensor(
                        zr[0:n, g, c0:c0 + m * E].rearrange("p (b e) -> p b e", b=m),
                        lex[0:n, g, :].unsqueeze(1).to_broadcast([n, m, E]), rrec[0:n, g:g + 1],
                        const[0:n, C_ZM:C_ZM + m].unsqueeze(2).to_broadcast([n, m, E]), ALU.mult, ALU.mult)
                last.then_inc(z_done, 1)

            TOPK_STEPS = 10

            def best_eight(k):
                r = slice(0, SET_ROWS[k])
                dve.wait_ge(route_ps, k + 1)
                nc.vector.max(top[r, k, 0, :], bank[ROUTE_BANK][r, 0:S]).then_inc(topk_done, 1)

            def without_best_eight(k):
                r = slice(0, SET_ROWS[k])
                dve.wait_ge(topk_done, TOPK_STEPS * k + 1)
                nc.vector.match_replace(rv2[r, k, :], top[r, k, 0, :], bank[ROUTE_BANK][r, 0:S],
                                        -1.0).then_inc(topk_done, 1)

            def next_eight(k):
                r = slice(0, SET_ROWS[k])
                dve.wait_ge(topk_done, TOPK_STEPS * k + 2)
                nc.vector.max(top[r, k, 1, :], rv2[r, k, :]).then_inc(topk_done, 1)

            def compare_with_least(k):
                r = slice(0, SET_ROWS[k])
                least = top[r, k, 1, CAP - 9:CAP - 8]
                dve.wait_ge(topk_done, TOPK_STEPS * k + 3)
                nc.vector.tensor_scalar(isgt[r, k, :], bank[ROUTE_BANK][r, 0:S], least, 0.0, ALU.is_gt, ALU.add,
                                        accum_out=ngt[r, k:k + 1]).then_inc(topk_done, 1)
                nc.vector.tensor_scalar(iseq[r, k, :], bank[ROUTE_BANK][r, 0:S], least, None,
                                        ALU.is_equal).then_inc(topk_done, 1)

            def rank_equals(k):
                r = slice(0, SET_ROWS[k])
                dve.wait_ge(topk_done, TOPK_STEPS * k + 5)
                nc.vector.tensor_tensor_scan(ceq[r, k, :], iseq[r, k, :], iseq[r, k, :], ngt[r, k:k + 1], ALU.add,
                                             ALU.bypass).then_inc(topk_done, 1)

            def equals_that_fit(k):
                r = slice(0, SET_ROWS[k])
                dve.wait_ge(topk_done, TOPK_STEPS * k + 6)
                nc.vector.scalar_tensor_tensor(fits[r, k, :], ceq[r, k, :], float(CAP), iseq[r, k, :], ALU.is_le,
                                               ALU.mult).then_inc(topk_done, 1)

            def count_picked(k):
                r = slice(0, SET_ROWS[k])
                dve.wait_ge(topk_done, TOPK_STEPS * k + 7)
                nc.vector.tensor_tensor_scan(cpick[r, k, :], fits[r, k, :], isgt[r, k, :], 0.0, ALU.add,
                                             ALU.add).then_inc(topk_done, 1)
                nc.vector.tensor_tensor(picked[r, k, :], fits[r, k, :], isgt[r, k, :], ALU.add).then_inc(topk_done, 1)

            def slot_numbers(k):
                r = slice(0, SET_ROWS[k])
                dve.wait_ge(topk_done, TOPK_STEPS * k + 9)
                nc.vector.tensor_tensor(slot[r, k, :], cpick[r, k, :], picked[r, k, :], ALU.mult).then_inc(topk_done, 1)

            def spread_slots(k):
                a, b = SETS[k]
                r, n, nb = slice(0, SET_ROWS[k]), SET_ROWS[k], SET_ROWS[k] // E
                dve.wait_ge(topk_done, TOPK_STEPS * k + 10)
                nc.vector.tensor_tensor(lall[r, a * GB:a * GB + nb, :], slot[r, k, :].unsqueeze(1).to_broadcast([n, nb, S]),
                                        const[r, C_LM:C_LM + nb].unsqueeze(2).to_broadcast([n, nb, S]),
                                        ALU.mult).then_inc(lall_done, 1)

            def select(g):
                k = 0 if g < SETS[0][1] else 1
                dve.wait_ge(slot_ps, k + 1)
                n, m, c0 = rows(g), pics(g) * CAP, (g - SETS[k][0]) * E
                nc.vector.tensor_tensor(sel[0:n, g, 0:E * m].rearrange("p (e s) -> p e s", e=E),
                                        bank[ROUTE_BANK][0:n, c0:c0 + E].unsqueeze(2).to_broadcast([n, E, m]),
                                        const[0:n, C_PAT:C_PAT + m].unsqueeze(1).to_broadcast([n, E, m]),
                                        ALU.is_equal).then_inc(sel_done, 1)

            def take_tokens(g):
                dve.wait_ge(gather_ps, g + 1)
                n = pics(g) * CAP
                nc.vector.tensor_copy(tokT[:, :, :, g * GB * CAP:g * GB * CAP + n],
                                      bank[GATHER_BANK[g]][:, 0:2 * E * n].rearrange("p (c e s) -> p c e s", c=2, e=E)
                                      ).then_inc(gather_dve, 1)

            def take_gates(r):
                dve.wait_ge(sgt_ps, r + 1)
                for k in range(4):
                    q, g = k // 2, 2 * r + k % 2
                    n, m = rows(g), 4 * pics(g) * CAP
                    last = nc.vector.tensor_copy(sgT[0:m, q, g, 0:n], bank[GATE_BANK[r]][0:m, k * GT:k * GT + n])
                last.then_inc(sgt_done, 1)

            nc.vector.memset(shared[:, 0:WARM], 0.0).then_inc(warm_ready, 1)
            norm_stats(0, 0)
            norm_stats(1, 0)
            norm_apply(0, 0)
            norm_stats(2, 0)
            norm_apply(1, 0)
            norm_apply(2, 0)
            norm_stats(3, 0)
            norm_apply(3, 0)
            norm_stats(4, 0)
            spread_k(0)
            take_v(0)
            norm_apply(4, 0)
            norm_stats(5, 0)
            subtract_max(0)
            norm_apply(5, 0)
            take_v(1)
            spread_k(1)
            subtract_max(1)
            divide(0)
            take_v(2)
            subtract_max(2)
            divide(1)
            take_v(3)
            for p in range(3, 7):
                subtract_max(p)
                divide(p - 1)
                if p >= 4:
                    norm_apply(p - 4, 1)
                take_v(p + 1)
                if p == 3:
                    spread_k(2)
                if p < 6:
                    norm_stats(p - 3, 1)
            subtract_max(7)
            router_max(0)
            weight_sums(6)
            router_shift(0)
            divide_y(6)
            router_sum(0)
            add_rows(3, 1)
            router_reciprocal(0)
            row_stats(3, 1)
            router_columns(0)
            mean_var(3, 1)
            router_divide(0)
            best_eight(0)
            var_eps(3, 1)
            without_best_eight(0)
            next_eight(0)
            compare_with_least(0)
            weight_sums(7)
            rank_equals(0)
            divide_y(7)
            equals_that_fit(0)
            newton_square(3, 1)
            count_picked(0)
            newton_factor(3, 1)
            slot_numbers(0)
            newton_apply(3, 1)
            spread_slots(0)
            normalise(3, 1)
            add_rows(4, 1)
            select(0)
            row_stats(4, 1)
            select(1)
            mean_var(4, 1)
            select(2)
            var_eps(4, 1)
            add_rows(5, 1)
            row_stats(5, 1)
            newton_square(4, 1)
            mean_var(5, 1)
            newton_factor(4, 1)
            var_eps(5, 1)
            newton_apply(4, 1)
            normalise(4, 1)
            newton_square(5, 1)
            newton_factor(5, 1)
            newton_apply(5, 1)
            normalise(5, 1)
            take_tokens(1)
            router_max(1)
            router_shift(1)
            router_sum(1)
            router_reciprocal(1)
            router_columns(1)
            router_divide(1)
            best_eight(1)
            without_best_eight(1)
            next_eight(1)
            compare_with_least(1)
            rank_equals(1)
            equals_that_fit(1)
            count_picked(1)
            slot_numbers(1)
            spread_slots(1)
            select(3)
            select(4)
            select(5)
            take_gates(0)
            take_tokens(3)
            take_tokens(5)
            take_gates(1)
            take_gates(2)

            def take_ye(e):
                for c in range(2):
                    dve.wait_ge(f2_ps, 2 * e + c + 1)
                    bias = b2s[:, 2 * e + c:2 * e + c + 1]
                    full, m, w = (G - 1) * GB * CAP, GB * CAP, pics(G - 1) * CAP
                    nc.vector.tensor_scalar(
                        yeT[:, c, e // 4, 0:4 * full].rearrange("p (g e s) -> p g e s", g=G - 1, e=4)[:, :, e % 4, :],
                        bank[F2_BANK[c]][:, 0:full].rearrange("p (g s) -> p g s", s=m), bias, None, ALU.add)
                    nc.vector.tensor_scalar(yeT[:, c, e // 4, 4 * full + e % 4 * w:4 * full + (e % 4 + 1) * w],
                                            bank[F2_BANK[c]][:, full:SLOTS], bias, None, ALU.add).then_inc(ye_done, 1)

            def add_out(q, g):
                n = rows(g)
                dve.wait_ge(sc_ps, q * G + g + 1)
                if q == 1:
                    dve.wait_ge(ob_done, g + 1)
                nc.vector.tensor_tensor(ob[0:n, g, :], bank[SC_BANK[q][g]][0:n, 0:D],
                                        (h if q == 0 else ob)[0:n, g, :], ALU.add).then_inc(ob_done, 1)

            dve.wait_ge(in_b, 32)
            for e in range(E):
                if e == 4:
                    for g in range(G + 2):
                        if g < G:
                            dve.wait_ge(yq_ps, g + 1)
                            n = 4 * pics(g) * CAP
                            nc.vector.tensor_copy(yq[0:n, g, :], bank[YQ_BANK[0][g]][0:n, 0:D]).then_inc(yq_dve, 1)
                        if g >= 2:
                            add_out(0, g - 2)
                take_ye(e)
            for g in range(G):
                add_out(1, g)

        @block.tensor
        def _(pe):
            def mm(out_, lhsT, rhs, start=True, stop=True, **kw):
                return nc.tensor.matmul(out_, lhsT, rhs, start=start, stop=stop, **kw)

            def warm_up():
                pe.wait_ge(warm_ready, 1)
                for _ in range(WARM_UP):
                    mm(bank[WARM_BANK][:, 0:WARM], shared[:, 0:128], shared[:, 0:WARM])

            def keep_warm(n, free):
                for _ in range(n):
                    mm(bank[free][:, 0:128], ident, ident)

            def patches(g):
                n = rows(g)
                pe.wait_ge(in_xp[g], 16)
                if g >= 2:
                    pe.wait_ge(h_done, g - 1)
                x = xps[:, KF * GT * g:KF * GT * g + KF * n].rearrange("p (k t) -> p k t", k=KF)
                for k in range(KF):
                    if g == 0 and k % 2 == 0:
                        pe.wait_ge(in_wl[k // 2], 16)
                    last = mm(bank[PATCH_BANK[g]][0:n, 0:D], x[:, k, :], wls[:, k, :], k == 0, k == KF - 1)
                last.then_inc(patch_done, 1)

            def transpose_rows(g, norm):
                n = rows(g)
                pe.wait_ge(xn_done, norm * G + g + 1)
                if norm == 0:
                    if g == 0:
                        pe.wait_ge(in_const, 16)
                    if g == 4:
                        pe.wait_ge(q_done, 2)
                    if g == 5:
                        pe.wait_ge(k_done, 2)
                elif g == 0:
                    pe.wait_ge(k_done, UNITS)
                elif g < 3:
                    pe.wait_ge(xnt_done, G + g)
                elif g == 3:
                    pe.wait_ge(sub_done, PAIRS)
                else:
                    pe.wait_ge(h_done, G + g + 1)
                for c in range(2):
                    last = mm(bank[T_BANK[norm][g]][:, c * n:c * n + n], xn[0:n, g, c * 128:c * 128 + 128],
                              ident[0:n, 0:n], is_transpose=True)
                last.then_inc(xnt_ps, 1)

            def project(u, which, dst, done):
                n = unit_rows(u)
                t0 = 2 * GT * u
                pe.wait_ge(xnt_done, 2 * u + 2)
                if u == 1:
                    pe.wait_ge(h_done, 5 + which)
                if u == 0:
                    pe.wait_ge(in_bd, 16)
                for c in range(2):
                    last = mm(bank[dst][:, c * n:c * n + n], bds[:, which, :], xnT[:, c, t0:t0 + n])
                last.then_inc(done, 1)

            def project_q(u):
                project(u, 0, Q_BANK[u], q_ps)

            def project_k(u):
                project(u, 1, K_BANK[u], k_ps)

            def values(p):
                pe.wait_ge(xnt_done, min(G, (2 * p + 1) // GB + 1))
                if p >= 1:
                    pe.wait_ge(vb_done, p)
                for b in range(2):
                    dst = bank[V_BANK][0:GT, b * D:b * D + D].rearrange("p (f c r) -> p c f r", f=2, c=2)
                    for c in range(2):
                        last = mm(dst[:, c, :, :], xn3[:, c, 2 * p + b, :], bds[:, 2, :])
                last.then_inc(v_ps, 1)

            def scores(p):
                if p == 0:
                    pe.wait_ge(constb_ready, 1)
                else:
                    pe.wait_ge(sub_done, p)
                u = 2 * p // (2 * GB)
                pe.wait_ge(q_done, u + 1)
                pe.wait_ge(km_done, 4 * (u + 1))
                for f in range(2):
                    for b in range(2):
                        mm(bank[S_BANK[f]][64 * b:64 * b + 64, 0:8 * S], id64b[64 * f:64 * f + S, :],
                           causalb[64 * f:64 * f + S, :], True, False, skip_group_check=True)
                for c in range(2):
                    for f in range(2):
                        for b in range(2):
                            t = (2 * p + b) * S
                            last = mm(bank[S_BANK[f]][64 * b:64 * b + 64, 4 * S * c:4 * S * (c + 1)],
                                      qT[64 * f:64 * f + 64, c, 2 * p + b, :], km[64 * f:64 * f + 64, c, :, t:t + S],
                                      False, c == 1, skip_group_check=True)
                last.then_inc(s_ps, 1)

            def transpose_weights(p):
                pe.wait_ge(exp_done, p + 1)
                if p == 0:
                    pe.wait_ge(empty_heads_ready, 1)
                    pe.wait_ge(xnt_done, 3)
                else:
                    pe.wait_ge(pt_done, 2 * p)
                for t in range(TRIPLES):
                    last = mm(bank[P_BANK[t // 4]][0:GT, 128 * (t % 4):128 * (t % 4) + 128],
                              pr[:, p % 2, 3 * t:3 * t + 3, :], ident, is_transpose=True)
                last.then_inc(pt_ps, 1)

            def weigh_values(p):
                pe.wait_ge(pt_done, 2 * p + 2)
                pe.wait_ge(vb_done, p + 1)
                if p == 0:
                    pe.wait_ge(ones_ready, 1)
                    pe.wait_ge(xnt_done, 4)
                else:
                    pe.wait_ge(yt_done, p)
                for t in range(TRIPLES):
                    m = min(3, HEADS - 3 * t)
                    for b in range(2):
                        last = mm(bank[Y_BANK][64 * b:64 * b + 64, 3 * t * VC:(3 * t + m) * VC],
                                  pT[0:GT, p % 2, t, 64 * b:64 * b + 64], vb[0:GT, p % 2, b, 3 * t:3 * t + m, :])
                last.then_inc(pv_ps, 1)

            def transpose_y(p):
                pe.wait_ge(y_done, p + 1)
                for c in range(2):
                    last = mm(bank[Y_BANK][:, c * 128:c * 128 + 128], ys[:, p % 2, 8 * c:8 * c + 8, :], ident,
                              is_transpose=True)
                last.then_inc(yt_ps, 1)

            def attention_out(g):
                n = rows(g)
                if g == 0:
                    pe.wait_ge(in_wu, 16)
                    pe.wait_ge(q_done, UNITS)
                elif g < 5:
                    pe.wait_ge(h_done, G + g)
                else:
                    pe.wait_ge(lsh_done, 1)
                pe.wait_ge(yt_done, pair_needs(g))
                for c in range(2):
                    last = mm(bank[O_BANK[g]][0:n, 0:D], yT[:, c, g * GT:g * GT + n], wus[:, c, :], c == 0, c == 1)
                last.then_inc(o_ps, 1)

            def route(g):
                k = 0 if g < SETS[0][1] else 1
                pe.wait_ge(xnt_done, G + g + 1)
                if g == 0:
                    pe.wait_ge(in_rw, 16)
                if g == SETS[1][0]:
                    pe.wait_ge(yt_done, PAIRS)
                if g == G - 1:
                    pe.wait_ge(xnT_pad_ready, 1)
                c0 = LOGIT_COL + (g - SETS[k][0]) * E
                for c in range(2):
                    last = mm(bank[LOGIT_BANK[k]][0:GT, c0:c0 + E], xnT[:, c, g * GT:g * GT + GT], rws[:, c, :],
                              c == 0, c == 1)
                last.then_inc(logit_ps, 1)

            def spread_router(k):
                a, b = SETS[k]
                pe.wait_ge(z_done, k + 1)
                pe.wait_ge(vb_done, PAIRS)
                if k == 1:
                    pe.wait_ge(sel_done, a)
                for g in range(a, b):
                    last = mm(bank[ROUTE_BANK][0:SET_ROWS[k], 0:S], zr[0:rows(g), g, 0:SET_ROWS[k]],
                              const[0:rows(g), C_D38:C_D38 + S], g == a, g == b - 1)
                last.then_inc(route_ps, 1)

            def slots_back(k):
                a, b = SETS[k]
                pe.wait_ge(lall_done, k + 1)
                for g in range(a, b):
                    m = pics(g)
                    last = mm(bank[ROUTE_BANK][0:rows(g), (g - a) * E:(g - a + 1) * E],
                              lall[0:SET_ROWS[k], GB * g:GB * g + m, :], e8b[0:SET_ROWS[k], :])
                last.then_inc(slot_ps, 1)

            def gather(g):
                n, m = rows(g), pics(g) * CAP
                pe.wait_ge(sel_done, g + 1)
                if g == 1:
                    pe.wait_ge(xnt_done, G + 4)
                if g == 2:
                    pe.wait_ge(pt_done, 2 * PAIRS)
                if g == 3:
                    pe.wait_ge(xnt_done, G + 5)
                if g == 4:
                    pe.wait_ge(sel_done, G)
                if g == 5:
                    pe.wait_ge(lsh_done, 2)
                for c in range(2):
                    last = mm(bank[GATHER_BANK[g]][:, c * E * m:c * E * m + E * m], xn[0:n, g, c * 128:c * 128 + 128],
                              sel[0:n, g, 0:E * m])
                last.then_inc(gather_ps, 1)

            chunks = [0]

            def chunk1(e, c, a, b):
                i = chunks[0]
                chunks[0] += 1
                if i >= 4:
                    pe.wait_ge(gelu_done, i - 3)
                for k in range(2):
                    last = mm(bank[F1_BANK[i % 4]][:, 0:b - a], w1s[:, e % NBUF, k, c * 128:c * 128 + 128],
                              tokT[:, k, e, a:b], k == 0, k == 1)
                last.then_inc(f1_ps, 1)

            def layer2(e):
                pe.wait_ge(in_w2[e % NBUF], 16 * (e // NBUF + 1))
                pe.wait_ge(gelu_done, f1_count(e))
                if e == 4:
                    pe.wait_ge(ob_done, G - 1)
                for c in range(2):
                    if e >= 1:
                        pe.wait_ge(ye_done, 2 * e - 1 + c)
                    for k in range(NH):
                        last = mm(bank[F2_BANK[c]][:, 0:SLOTS], w2s[:, e % NBUF, k, c * 128:c * 128 + 128],
                                  gT[:, e % 2, k, :], k == 0, k == NH - 1)
                    last.then_inc(f2_ps, 1)

            def transpose_gates(r):
                if r == 0:
                    pe.wait_ge(h_done, 2 * G)
                    pe.wait_ge(xnt_done, 2 * G)
                if r == 1:
                    pe.wait_ge(gather_dve, 2)
                if r == 2:
                    pe.wait_ge(sgt_done, 1)
                for k in range(4):
                    q, g = k // 2, 2 * r + k % 2
                    n, m = rows(g), pics(g) * CAP
                    pe.wait_ge(selg_done, g + 1)
                    last = mm(bank[GATE_BANK[r]][0:4 * m, k * GT:k * GT + n], selg[0:n, g, 4 * q * m:4 * (q + 1) * m],
                              ident[0:n, 0:n], is_transpose=True)
                last.then_inc(sgt_ps, 1)

            def transpose_ye(q, g, c):
                m = pics(g) * CAP
                return mm(bank[YQ_BANK[q][g]][0:4 * m, c * 128:c * 128 + 128],
                          yeT[:, c, q, 4 * g * GB * CAP:4 * g * GB * CAP + 4 * m], ident, is_transpose=True)

            def scatter(q, g):
                n, m = rows(g), 4 * pics(g) * CAP
                mm(bank[SC_BANK[q][g]][0:n, 0:D], sgT[0:m, q, g, 0:n], yq[0:m, g, :]).then_inc(sc_ps, 1)

            warm_up()
            patches(0)
            patches(1)
            patches(2)
            transpose_rows(0, 0)
            patches(3)
            transpose_rows(1, 0)
            patches(4)
            project_q(0)
            project_k(0)
            transpose_rows(2, 0)
            transpose_rows(3, 0)
            values(0)
            patches(5)
            scores(0)
            values(1)
            project_q(1)
            project_k(1)
            transpose_weights(0)
            scores(1)
            weigh_values(0)
            values(2)
            transpose_rows(4, 0)
            transpose_y(0)
            transpose_weights(1)
            transpose_rows(5, 0)
            scores(2)
            weigh_values(1)
            values(3)
            project_q(2)
            transpose_y(1)
            transpose_weights(2)
            for p in range(3, 7):
                scores(p)
                weigh_values(p - 1)
                if p >= 5:
                    route(p - 5)
                values(p + 1)
                if p == 3:
                    project_k(2)
                transpose_y(p - 1)
                transpose_weights(p)
                if p >= 4:
                    transpose_rows(p - 4, 1)
                if p < 6:
                    attention_out(p - 3)
            scores(7)
            route(2)
            weigh_values(6)
            attention_out(3)
            transpose_weights(7)
            transpose_y(6)
            keep_warm(2, S_BANK[0])
            spread_router(0)
            weigh_values(7)
            keep_warm(4, P_BANK[1])
            transpose_y(7)
            keep_warm(2, P_BANK[1])
            attention_out(4)
            slots_back(0)
            attention_out(5)
            transpose_rows(3, 1)
            gather(0)
            route(3)
            gather(1)
            keep_warm(2, P_BANK[1])
            transpose_rows(4, 1)
            gather(2)
            transpose_rows(5, 1)
            route(4)
            route(5)
            pe.wait_ge(in_w1[0], 16)
            pe.wait_ge(gather_act, 2)
            pe.wait_ge(gather_dve, 1)
            for c in range(4):
                chunk1(0, c, 0, SLOTS_A)
            spread_router(1)
            for c in range(4, NH):
                chunk1(0, c, 0, SLOTS_A)
            slots_back(1)
            transpose_gates(0)
            gather(3)
            gather(4)
            gather(5)
            transpose_gates(1)
            transpose_gates(2)
            pe.wait_ge(in_w1[1], 16)
            pe.wait_ge(gather_act, 3)
            pe.wait_ge(gather_dve, 3)
            for c in range(NH):
                chunk1(0, c, SLOTS_A, SLOTS)
                chunk1(1, c, 0, SLOTS)
            for e in range(E):
                if 1 <= e < E - 1:
                    pe.wait_ge(in_w1[(e + 1) % NBUF], 16 * ((e + 1) // NBUF + 1))
                    for c in range(NH):
                        chunk1(e + 1, c, 0, SLOTS)
                        if e == 4 and c == 0:
                            pe.wait_ge(sgt_done, 3)
                            pe.wait_ge(ye_done, 8)
                        if e == 4 and 2 <= c < G + 2:
                            pe.wait_ge(yq_dve, c - 1)
                            if c >= 4:
                                pe.wait_ge(ob_done, c - 3)
                            scatter(0, c - 2)
                        if e == 4 and c < G:
                            if c >= 2:
                                pe.wait_ge(yq_dve, c - 1)
                            transpose_ye(0, c, 0)
                            transpose_ye(0, c, 1).then_inc(yq_ps, 1)
                layer2(e)
            pe.wait_ge(gelu_done, f1_count(E - 1))
            pe.wait_ge(ob_done, G)
            pe.wait_ge(ye_done, 2 * E - 1)
            for g in range(G):
                transpose_ye(1, g, 0)
            pe.wait_ge(ye_done, 2 * E)
            for g in range(G):
                transpose_ye(1, g, 1).then_inc(yq_ps, 1)
            for g in range(G):
                pe.wait_ge(yq_act, max(g + 1, 3 if g >= 2 else 0))
                if g >= 4:
                    pe.wait_ge(ob_done, G + g - 3)
                scatter(1, g)


def shape_constants():
    import numpy as np
    c = np.zeros((128, C_END), np.float32)
    p = np.arange(128)
    c[:, C_ID:C_ID + 128] = np.eye(128)
    for m in range(4):
        c[:, C_KM + m] = 0.25 * ((p % 64) // HC == m)
    for i in range(HEADS):
        c[:, C_M3 + i] = p // S == i % 3
    for b in range(GB):
        for s in range(CAP):
            c[:, C_PAT + b * CAP + s] = np.where(p // S == b, s + 1, -1)
        c[:, C_ZM + b] = p // S == b
    for s in range(S):
        c[:, C_D38 + s] = p % S == s
    for b in range(SETS[0][1] * GB):
        c[:, C_LM + b] = p // E == b
    for e in range(E):
        c[:, C_E8 + e] = p % E == e
    for r in (0, 64):
        for i in range(S):
            c[r + i, C_I64 + i] = 1
    for r in (0, 64):
        for i in range(S):
            for hd in range(8):
                c[r + i, C_CM + hd * S + i + 1:C_CM + hd * S + S] = MASKED
    return c


def kernel(x, cls_tok, L0_tok_W_lin, L0_tok_b_lin, L0_tok_class_token, L0_tok_position_embeddings, L0_attn_Wq,
           L0_attn_Wk, L0_attn_Wv, L0_attn_Wu, L0_attn_bu, L0_ffn_router_w, L0_ffn_w1, L0_ffn_b1, L0_ffn_w2,
           L0_ffn_b2):
    import numpy as np
    import concourse.bacc as bacc
    from concourse.bass_utils import run_bass_kernel_spmd

    a = lambda v: np.ascontiguousarray(np.asarray(v))
    side = IMG // PATCH
    xf = a(x).reshape(B, C_IN, side, PATCH, side, PATCH).transpose(1, 3, 5, 0, 2, 4).reshape(F, B, NPATCH)
    xt = np.zeros((F, B, S), np.float32)
    xt[:, :, 2:] = xf
    xt = xt.reshape(KF, 128, TOK)
    xp = np.concatenate([xt[:, :, g * GT:g * GT + rows(g)].transpose(1, 0, 2).reshape(128, -1) for g in range(G)], axis=1)
    wl = a(L0_tok_W_lin).T.reshape(KF, 128, D).transpose(1, 0, 2)
    one_a = np.concatenate([a(cls_tok).reshape(1, D), a(L0_tok_position_embeddings).reshape(S - 1, D)])
    one_b = np.concatenate([np.zeros((1, D), np.float32), a(L0_tok_class_token).reshape(1, D),
                            np.repeat(a(L0_tok_b_lin).reshape(1, D), NPATCH, axis=0)])
    rows_a, rows_b = (np.resize(v, (128, D)) for v in (one_a, one_b))
    bd = np.zeros((128, 3, 128), np.float32)
    for w, m in enumerate((L0_attn_Wq, L0_attn_Wk, L0_attn_Wv)):
        for i in range(128 // HC):
            bd[i * HC:(i + 1) * HC, w, i * HC:(i + 1) * HC] = a(m).T
    wu = a(L0_attn_Wu).T.reshape(2, 128, D).transpose(1, 0, 2)
    bu = np.repeat(a(L0_attn_bu).reshape(1, D), 128, axis=0)
    rw = a(L0_ffn_router_w).T.reshape(2, 128, E).transpose(1, 0, 2)
    w1 = a(L0_ffn_w1).reshape(E, 2, 128, HID).transpose(0, 2, 1, 3)
    b1 = a(L0_ffn_b1).reshape(E * NH, 128).T
    w2 = a(L0_ffn_w2).reshape(E, NH, 128, D).transpose(0, 2, 1, 3)
    b2 = a(L0_ffn_b2).reshape(E * 2, 128).T
    arrays = dict(xp=xp, wl=wl, rows_a=rows_a, rows_b=rows_b, bd=bd, wu=wu, bu=bu, rw=rw, w1=w1, b1=b1, w2=w2, b2=b2,
                  consts=shape_constants())
    arrays = {f"{n}_dram": np.ascontiguousarray(v) for n, v in arrays.items()}

    nc = bacc.Bacc("TRN2", target_bir_lowering=False, num_devices=1)
    args = [nc.dram_tensor(n, v.shape, mybir.dt.float32, kind="ExternalInput").ap() for n, v in arrays.items()]
    out = nc.dram_tensor("out_dram", (TOK, D), mybir.dt.float32, kind="ExternalOutput").ap()
    tower(nc, *args, out)
    r = run_bass_kernel_spmd(nc, [arrays], core_ids=[0])
    return r.results[0]["out_dram"].reshape(B, S, D)
```
